# Optimizing a Trainium2 kernel written in Bass

```python
import numpy as np
import jax
import jax.numpy as jnp

def _softmax(x, axis=-1):
    return jax.nn.softmax(x, axis=axis)

def _gelu(x):
    return jax.nn.gelu(x, approximate=True)

def _silu(x):
    return jax.nn.silu(x)

def _sigmoid(x):
    return jax.nn.sigmoid(x)

def _layernorm(x, axis=-1, eps=1e-05):
    m = jnp.mean(x, axis=axis, keepdims=True)
    v = jnp.var(x, axis=axis, keepdims=True)
    return (x - m) / jnp.sqrt(v + eps)

def _scatter_add(tgt, idx, src, axis=0):
    return tgt.at[idx].add(src)

def _segment_sum(src, seg, n):
    return jax.ops.segment_sum(src, seg, n)
kernel_name = 'mk_conv_preact_d2_conv_nchw64_r2_4a0ae2'

def setup_inputs(seed: int=0):
    np.random.seed(seed)
    _w = jnp.asarray

    def _rec_inputs():
        import jax
        import jax.numpy as jnp
        _gk = jax.random.key(seed)
        x = 8.816e-06 + 1 * jax.random.normal(jax.random.fold_in(_gk, 1), (16, 32, 112, 112), jnp.float32)
        return x
    x = _rec_inputs()

    def _L0_conv_setup():
        import jax, jax.numpy as jnp
        import numpy as np

        def _dct2_matrix(n: int) -> jnp.ndarray:
            k = np.arange(n)[:, None].astype(np.float64)
            m = np.arange(n)[None, :].astype(np.float64)
            d = np.cos(np.pi * (2.0 * m + 1.0) * k / (2.0 * n))
            scale = np.full((n, 1), np.sqrt(2.0 / n))
            scale[0, 0] = np.sqrt(1.0 / n)
            return jnp.asarray((scale * d).astype(np.float32))
        key = jax.random.key(seed)
        x = jax.random.normal(key, (32, 32, 112, 112), dtype=jnp.float32)
        return {'x': x}
    _L0_conv_all = _L0_conv_setup()
    _L0_conv_in = {k: v for k, v in _L0_conv_all.items() if k in ()}
    del _L0_conv_all

    def _L1_conv_setup():
        import jax, jax.numpy as jnp
        import numpy as np
        B, C, H, W = (64, 32, 32, 32)
        GROUPS = 32
        EPS = 1e-05
        NUM_STEPS = 6
        T0, T1 = (0.0, 1.0)

        def _group_norm(x, w, b):
            bb, cc, hh, ww = x.shape
            xr = x.reshape(bb, GROUPS, cc // GROUPS, hh, ww)
            mu = xr.mean(axis=(2, 3, 4), keepdims=True)
            var = xr.var(axis=(2, 3, 4), keepdims=True)
            xn = (xr - mu) * jax.lax.rsqrt(var + EPS)
            xn = xn.reshape(bb, cc, hh, ww)
            return xn * w[None, :, None, None] + b[None, :, None, None]

        def _concat_conv(t, x, w, b):
            tt = jnp.full((x.shape[0], 1, x.shape[2], x.shape[3]), t, x.dtype)
            xt = jnp.concatenate([tt, x], axis=1)
            y = jax.lax.conv_general_dilated(xt, w, window_strides=(1, 1), padding=((1, 1), (1, 1)), dimension_numbers=('NCHW', 'OIHW', 'NCHW'))
            return y + b[None, :, None, None]
        key = jax.random.key(seed)
        k0, k1, k2 = jax.random.split(key, 3)
        fan_in = (C + 1) * 3 * 3
        scale = 1.0 / np.sqrt(fan_in)
        return {'x': jax.random.normal(k0, (B, C, H, W), jnp.float32), 'gn1_w': jnp.ones((C,), jnp.float32), 'gn1_b': jnp.zeros((C,), jnp.float32), 'conv1_w': jax.random.normal(k1, (C, C + 1, 3, 3), jnp.float32) * scale, 'conv1_b': jnp.zeros((C,), jnp.float32), 'gn2_w': jnp.ones((C,), jnp.float32), 'gn2_b': jnp.zeros((C,), jnp.float32), 'conv2_w': jax.random.normal(k2, (C, C + 1, 3, 3), jnp.float32) * scale, 'conv2_b': jnp.zeros((C,), jnp.float32), 'gn3_w': jnp.ones((C,), jnp.float32), 'gn3_b': jnp.zeros((C,), jnp.float32)}
    _L1_conv_all = _L1_conv_setup()
    _L1_conv_in = {k: v for k, v in _L1_conv_all.items() if k in ('gn1_w', 'gn1_b', 'conv1_w', 'conv1_b', 'gn2_w', 'gn2_b', 'conv2_w', 'conv2_b', 'gn3_w', 'gn3_b')}
    del _L1_conv_all
    return {'x': x, 'L1_conv_gn1_w': _L1_conv_in['gn1_w'], 'L1_conv_gn1_b': _L1_conv_in['gn1_b'], 'L1_conv_conv1_w': _L1_conv_in['conv1_w'], 'L1_conv_conv1_b': _L1_conv_in['conv1_b'], 'L1_conv_gn2_w': _L1_conv_in['gn2_w'], 'L1_conv_gn2_b': _L1_conv_in['gn2_b'], 'L1_conv_conv2_w': _L1_conv_in['conv2_w'], 'L1_conv_conv2_b': _L1_conv_in['conv2_b'], 'L1_conv_gn3_w': _L1_conv_in['gn3_w'], 'L1_conv_gn3_b': _L1_conv_in['gn3_b']}

def reference(x, L1_conv_gn1_w, L1_conv_gn1_b, L1_conv_conv1_w, L1_conv_conv1_b, L1_conv_gn2_w, L1_conv_gn2_b, L1_conv_conv2_w, L1_conv_conv2_b, L1_conv_gn3_w, L1_conv_gn3_b):
    import jax
    import jax.numpy as jnp

    def _L0_conv_ref(x):
        import jax, jax.numpy as jnp
        import numpy as np

        def _dct2_matrix(n: int) -> jnp.ndarray:
            k = np.arange(n)[:, None].astype(np.float64)
            m = np.arange(n)[None, :].astype(np.float64)
            d = np.cos(np.pi * (2.0 * m + 1.0) * k / (2.0 * n))
            scale = np.full((n, 1), np.sqrt(2.0 / n))
            scale[0, 0] = np.sqrt(1.0 / n)
            return jnp.asarray((scale * d).astype(np.float32))
        B, C, H, W = x.shape
        Dh = _dct2_matrix(H)
        Dw = _dct2_matrix(W)
        y = jnp.einsum('kh,bchw->bckw', Dh, x)
        y = jnp.einsum('lw,bckw->bckl', Dw, y)
        return y

    def _L1_conv_ref(x, gn1_w, gn1_b, conv1_w, conv1_b, gn2_w, gn2_b, conv2_w, conv2_b, gn3_w, gn3_b):
        import jax, jax.numpy as jnp
        import numpy as np
        B, C, H, W = (64, 32, 32, 32)
        GROUPS = 32
        EPS = 1e-05
        NUM_STEPS = 6
        T0, T1 = (0.0, 1.0)

        def _group_norm(x, w, b):
            bb, cc, hh, ww = x.shape
            xr = x.reshape(bb, GROUPS, cc // GROUPS, hh, ww)
            mu = xr.mean(axis=(2, 3, 4), keepdims=True)
            var = xr.var(axis=(2, 3, 4), keepdims=True)
            xn = (xr - mu) * jax.lax.rsqrt(var + EPS)
            xn = xn.reshape(bb, cc, hh, ww)
            return xn * w[None, :, None, None] + b[None, :, None, None]

        def _concat_conv(t, x, w, b):
            tt = jnp.full((x.shape[0], 1, x.shape[2], x.shape[3]), t, x.dtype)
            xt = jnp.concatenate([tt, x], axis=1)
            y = jax.lax.conv_general_dilated(xt, w, window_strides=(1, 1), padding=((1, 1), (1, 1)), dimension_numbers=('NCHW', 'OIHW', 'NCHW'))
            return y + b[None, :, None, None]

        def odefunc(t, y):
            h = jax.nn.relu(_group_norm(y, gn1_w, gn1_b))
            h = _concat_conv(t, h, conv1_w, conv1_b)
            h = jax.nn.relu(_group_norm(h, gn2_w, gn2_b))
            h = _concat_conv(t, h, conv2_w, conv2_b)
            return _group_norm(h, gn3_w, gn3_b)
        dt = (T1 - T0) / NUM_STEPS

        def step(y, t):
            return (y + dt * odefunc(t, y), None)
        ts = T0 + dt * jnp.arange(NUM_STEPS, dtype=x.dtype)
        y1, _ = jax.lax.scan(step, x, ts)
        return y1

    def _gn(v, G=32, eps=1e-05):
        B_, C_, H_, W_ = v.shape
        g = v.reshape(B_, G, C_ // G, H_, W_)
        m = jnp.mean(g, axis=(2, 3, 4), keepdims=True)
        s = jnp.var(g, axis=(2, 3, 4), keepdims=True)
        return ((g - m) / jnp.sqrt(s + eps)).reshape(v.shape)

    def _ln_c(v, eps=1e-06):
        m = jnp.mean(v, axis=1, keepdims=True)
        s = jnp.var(v, axis=1, keepdims=True)
        return (v - m) / jnp.sqrt(s + eps)

    def _ln_t(v, eps=1e-05):
        m = jnp.mean(v, axis=-1, keepdims=True)
        s = jnp.var(v, axis=-1, keepdims=True)
        return (v - m) / jnp.sqrt(s + eps)

    def _to_tokens(v):
        B_, C_, H_, W_ = v.shape
        return v.reshape(B_, C_, H_ * W_).transpose(0, 2, 1)

    def _from_tokens(t, like):
        B_, C_, H_, W_ = like.shape
        return t.transpose(0, 2, 1).reshape(B_, C_, H_, W_)
    x = x + _L0_conv_ref(_gn(x))
    x = x + _L1_conv_ref(_gn(x), L1_conv_gn1_w, L1_conv_gn1_b, L1_conv_conv1_w, L1_conv_conv1_b, L1_conv_gn2_w, L1_conv_gn2_b, L1_conv_conv2_w, L1_conv_conv2_b, L1_conv_gn3_w, L1_conv_gn3_b)
    return x

_drawn_inputs = setup_inputs


def setup_inputs(seed=0):
    import zlib

    import numpy as np

    out = dict(_drawn_inputs(seed))
    spreads = {'L1_conv_gn1_w': (1.0, 0.2),
     'L1_conv_gn1_b': (0.0, 0.27),
     'L1_conv_conv1_b': (0.0, 0.8),
     'L1_conv_gn2_w': (1.0, 0.2),
     'L1_conv_gn2_b': (0.0, 0.276),
     'L1_conv_conv2_b': (0.0, 0.8),
     'L1_conv_gn3_w': (1.0, 0.2),
     'L1_conv_gn3_b': (0.0, 0.1)}
    factors = {}
    for name, (base, spread) in spreads.items():
        noise = np.random.default_rng([zlib.crc32(name.encode()), seed]).standard_normal(out[name].shape)
        drawn = base * np.exp(spread * noise) if base else spread * noise
        out[name] = jnp.asarray(drawn.astype(out[name].dtype))
    for name, factor in factors.items():
        out[name] = (out[name] * factor).astype(out[name].dtype)
    return out
```

```python
from contextlib import ExitStack

import numpy as np

import concourse.bass as bass
from concourse import mybir

F32 = mybir.dt.float32
F16 = mybir.dt.float16
I32 = mybir.dt.int32
ALU = mybir.AluOpType
ACT = mybir.ActivationFunctionType
AX_X = mybir.AxisListType.X
RMAX = bass.bass_isa.ReduceOp.max

C = 32
H = 112
NA = H // 2
NB = NA + 1
PADA = NA + 2
PB = NB + 1
SLOTS = 2
STEPS = 6
DT = 1.0 / STEPS
EPS = 1e-5
BANKS = 5
TILES1 = [8] + [7] * 7
TILES2 = [8] * 7
PARTS_A = [14] * 4
PARTS_B = [15, 14, 14, 14]
NP = 4
CQ = C // 2
NBATCH = CQ // 4
PIECE = CQ * H * H // 128

Z1, Z2, Y, IZ, IY, X0 = range(6)
MID, FOUR, FIVE = range(3)
STATS = {
    MID: [(Z1, 0), (X0, 0), (Z1, 1), (Z2, 0), (Y, 0), (Z2, 1), (Y, 1)],
    FOUR: [(Z1, 0), (IZ, 0), (Z1, 1), (Z2, 0), (IZ, 1), (Y, 0), (IY, 0), (Z2, 1), (Y, 1)],
    FIVE: [(Z1, 0), (IY, 1), (Z1, 1), (Z2, 0), (Z2, 1)],
}
POSTS = {k: [e for e in v if e[0] != X0] for k, v in STATS.items()}
PRES = {MID: [(Z1, 0), (Z1, 1), (Z2, 0), (Z2, 1)],
        FOUR: [(Z1, 0), (IZ, 0), (Z1, 1), (IZ, 1), (Z2, 0), (Z2, 1)],
        FIVE: [(Z1, 0), (Z1, 1), (Z2, 0), (Z2, 1)]}
NPOST = 4
NHALF_STEPS = 10
MEAN, E2, MS, ES, VAR, VE, RSTD, SC, BI = range(9)
G1, B1, G2, B2, G3, B3, CB1, CB2 = range(8)
LO_ROW = 32


def offsets(rows):
    return [sum(rows[:k]) for k in range(len(rows))]


def dct_matrix():
    k = np.arange(H)[:, None].astype(np.float64)
    m = np.arange(H)[None, :].astype(np.float64)
    d = np.cos(np.pi * (2.0 * m + 1.0) * k / (2.0 * H))
    scale = np.full((H, 1), np.sqrt(2.0 / H))
    scale[0, 0] = np.sqrt(1.0 / H)
    return (scale * d).astype(np.float32)


def constants():
    d = dct_matrix()
    dct = np.stack([d.T, d.T.reshape(H, NA, 2).transpose(0, 2, 1).reshape(H, H)], axis=1)
    p = np.arange(128)
    same = (p[:, None] % C == p[None, :] % C).astype(np.float32)
    mats = np.zeros((128, 3, 128), np.float32)
    mats[:, 0] = same / 4
    mats[:, 1] = same / (H * H)
    mats[:, 2] = 0.5 / H
    coef = np.zeros((128, 2, 4, 128), np.float32)
    for conv in range(2):
        for q in range(4):
            rx, ry = q // 2, q % 2
            top, left = (ry == 1, rx == 1) if conv == 0 else (ry == 0, rx == 0)
            for ky in range(3):
                for kx in range(3):
                    row = [0.0] * 8
                    if top and ky == 0:
                        row[0] = -1.0
                        row[1] = float(left and kx == 0)
                        row[2] = float(not left and kx == 2)
                    if not top and ky == 2:
                        row[3] = -1.0
                        row[4] = float(left and kx == 0)
                        row[5] = float(not left and kx == 2)
                    row[6] = -float(left and kx == 0)
                    row[7] = -float(not left and kx == 2)
                    coef[3 * ky + kx, conv, q, 0:8] = row
                    coef[3 * ky + kx, conv, q, LO_ROW:LO_ROW + 8] = row
    ind = np.zeros((128, RIM), np.float16)
    for n, at in ((NB, RIM1), (NA, RIM2)):
        for base in (0, LO_ROW):
            ind[base, at:at + n] = 1
            ind[base + 1, at] = 1
            ind[base + 2, at + n - 1] = 1
            ind[base + 3, at + n:at + 2 * n] = 1
            ind[base + 4, at + n] = 1
            ind[base + 5, at + 2 * n - 1] = 1
    for base in (0, LO_ROW):
        ind[base + 6, RIMC::2] = 1
        ind[base + 7, RIMC + 1::2] = 1
    return dct, mats, coef, ind


RIM1, RIM2, RIMC = 0, 2 * NB, 2 * NB + 2 * NA
RIM = RIMC + 16


def build(nc, x, wt, w0, par, dct_c, mats_c, coef_c, ind_c, x1d, yd, out):
    B = x.shape[0]
    GROUPS = B // SLOTS
    NHALF = 2 * B
    HALVES = 2 * SLOTS

    with ExitStack() as ctx:
        def sb(name, shape, dt=F32):
            return ctx.enter_context(nc.sbuf_tensor(name, shape, dt))

        def pb(name):
            return ctx.enter_context(nc.psum_tensor(name, [128, 512], F32))

        def sem(name):
            return ctx.enter_context(nc.semaphore(name))

        y = [sb(f"y{s}", [128, NA * NA]) for s in range(SLOTS)]
        z = [sb(f"z{s}", [128, NB * NB]) for s in range(SLOTS)]
        ha = [sb(f"ha{s}", [128, 2, PADA * PADA], F16) for s in range(SLOTS)]
        hb = [sb(f"hb{s}", [128, 2, NB * PB], F16) for s in range(SLOTS)]
        xa = [sb(f"xa{s}", [128, NA * NA]) for s in range(SLOTS)]
        bn = [sb(f"bn{s}", [128, 10, 6]) for s in range(SLOTS)]
        bni = [sb(f"bni{s}", [128, 7, 6]) for s in range(SLOTS)]
        small = sb("small", [128, SLOTS, 5, 9])
        ysum = sb("ysum", [128, SLOTS, NP, 2])
        isum = sb("isum", [128, SLOTS, 2])
        shift = sb("shift", [128, SLOTS])
        xs = sb("xs", [H, CQ, H])
        xn = sb("xn", [H, CQ, H])
        ts = sb("ts", [H, 2, 4, H])
        x1s = sb("x1s", [H, CQ, 2, NA])
        bn0 = sb("bnx", [H, CQ, 6])
        m0 = sb("m0", [H, 6, 2 * CQ])
        fin = sb("fin", [128, 3, PIECE])
        w1 = sb("w1", [128, 4, 2, 128], F16)
        w2 = sb("w2", [128, 4, 2, 128], F16)
        rim_w = sb("rim_w", [128, 2, STEPS, 128], F16)
        rim_i = sb("rim_i", [128, RIM], F16)
        cbias = sb("cbias", [128, 2, STEPS])
        dct = sb("dct", [H, 2, H])
        mats = sb("mats", [128, 3, 128])
        prm = sb("prm", [128, 8])
        gb = sb("gb", [128, 8])
        half = sb("half", [128, CQ])
        epsc = sb("epsc", [128, 2])
        last_shift = sb("last_shift", [128, SLOTS])
        bias_now = sb("bias_now", [128, 2])
        zero = sb("zero", [128, 1])
        ones = sb("ones", [128, 1])

        cps = [pb(f"cps{i}") for i in range(BANKS)]
        sps = pb("sps")
        tps = pb("tps")
        xps = pb("xps")

        setup_in = sem("setup_in")
        s_set = sem("s_set")
        s_max = sem("s_max")
        s_rimps = sem("s_rimps")
        set_done = sem("set_done")
        pool_set = sem("pool_set")
        tile_done = sem("tile_done")
        evac_done = sem("evac_done")
        bn_done = sem("bn_done")
        pre_done = sem("pre_done")
        stat_done = sem("stat_done")
        stat_read = sem("stat_read")
        post_done = sem("post_done")
        pow_done = sem("pow_done")
        r_done = sem("r_done")
        hi_done = sem("hi_done")
        lo_done = sem("lo_done")
        rim_zero = sem("rim_zero")
        sp_gate = sem("sp_gate")
        bias_set = sem("bias_set")
        dve_gate = sem("dve_gate")
        pool_gate = sem("pool_gate")
        pz = sem("pz")
        yup_done = sem("yup_done")
        sq_done = sem("sq_done")
        fin_done = sem("fin_done")
        y_out = [sem(f"y_out{s}") for s in range(SLOTS)]
        y_new = [sem(f"y_new{s}") for s in range(SLOTS)]
        xa_in = [sem(f"xa_in{s}") for s in range(SLOTS)]
        ibn_done = sem("ibn_done")
        y0_done = sem("y0_done")
        isq_done = sem("isq_done")
        shift_set = sem("shift_set")
        xs_in = sem("xs_in")
        s_m0 = sem("s_m0")
        pow0 = sem("pow0")
        s_xn = sem("s_xn")
        t_done = sem("t_done")
        ts_done = sem("ts_done")
        xp_done = sem("xp_done")
        x1_done = sem("x1_done")
        x1_out = sem("x1_out")
        fin_in = sem("fin_in")
        add_done = sem("add_done")
        out_done = sem("out_done")

        def tiles_before(g, s):
            return 8 + 30 * (STEPS * g + s)

        def parts_before(g, s):
            return 2 * NP + 4 * NP * (STEPS * g + s)

        def events_before(table, first, g, s):
            mid, four, five = (len(table[k]) for k in (MID, FOUR, FIVE))
            in_group = 4 * mid + four if isinstance(s, int) and s == 5 else mid * s
            return first + (4 * mid + four + five) * g + in_group

        def stats_before(g, s):
            return events_before(STATS, HALVES + 2 * SLOTS, g, s)

        def posts_before(g, s):
            return events_before(POSTS, 2 * SLOTS, g, s)

        def pres_before(g, s):
            return events_before(PRES, SLOTS, g, s)

        x_half = x.rearrange("b (f c) h w -> (b f) h c w", f=2)
        x1_half = x1d.rearrange("b (f c) h r j -> (b f) h c (r j)", f=2)
        x1_piece = x1d.rearrange("b (f c) h r j -> (b f) (c h r j)", f=2).rearrange("a (p n) -> a p n", p=128)
        y_piece = yd.rearrange("b (f c) h r j -> (b f) (c h r j)", f=2).rearrange("a (p n) -> a p n", p=128)
        out_piece = out.rearrange("b (f c) h w -> (b f) (c h w)", f=2).rearrange("a (p n) -> a p n", p=128)

        def grid_a_in_dram(t, b, q):
            rx, ry = q // 2, q % 2
            v = t.rearrange("b c (i e) r j -> b e r c i j", e=2)
            if isinstance(b, int):
                return v[b, ry, rx]
            return v[bass.ds(b, 1), ry, rx].rearrange("b c i j -> (b c) i j")

        def col(t, slot, kind, k, n=1):
            return t[:, slot, kind, k:k + n]

        block = ctx.enter_context(nc.Block())

        @block.sync
        def _(sp):
            for dst, src in ((prm, par), (mats, mats_c), (rim_i, ind_c)):
                sp.dma_start(dst[:], src).then_inc(setup_in, 16)
            sp.dma_start(z[0][:, 0:2 * 9 * C], wt).then_inc(setup_in, 16)
            sp.dma_start(z[1][:, 0:256], w0).then_inc(setup_in, 16)
            sp.dma_start(z[1][:, 256:256 + 1024], coef_c).then_inc(setup_in, 16)
            sp.dma_start(dct[:], dct_c).then_inc(setup_in, 16)

            def load_half(index, n):
                sp.wait_ge(x1_done, NBATCH * n + 1)
                sp.dma_start(xs[:], x_half[bass.ds(index, 1)].rearrange("a h c w -> (a h) c w")).then_inc(xs_in, 16)

            def store_half(n):
                sp.wait_ge(x1_done, NBATCH * (n + 1) + 1)
                sp.dma_start(x1_half[bass.ds(n, 1)].rearrange("a h c w -> (a h) c w"),
                             x1s[:].rearrange("h c r j -> h c (r j)")).then_inc(x1_out, 16)

            def load_start(slot, b, halves):
                sp.wait_ge(x1_out, 16 * halves + 16)
                for q in range(4):
                    sp.dma_start(xa[slot][q * C:(q + 1) * C, :].rearrange("c (i j) -> c i j", j=NA),
                                 grid_a_in_dram(x1d, b, q)).then_inc(xa_in[slot], 16)

            def new_state(slot, n):
                sp.wait_ge(y0_done, n)
                sp.dma_start(y[slot][:], xa[slot][:]).then_inc(y_new[slot], 16)

            def last_piece(g, n):
                at = bass.ds((n + NHALF - HALVES) % NHALF, 1)
                sp.wait_ge(out_done, 16 * n + 16)
                sp.sem_inc(sp_gate, 1)
                sp.wait_ge(isq_done, SLOTS * (g + 1) + 1)
                sp.dma_start(fin[:, 0, :], x1_piece[at].rearrange("a p n -> (a p) n")).then_inc(fin_in, 16)
                sp.dma_start(fin[:, 1, :], y_piece[at].rearrange("a p n -> (a p) n")).then_inc(fin_in, 16)
                sp.wait_ge(add_done, n + 2)
                sp.dma_start(out_piece[at].rearrange("a p n -> (a p) n"),
                             fin[:, 2, :]).then_inc(out_done, 16)

            sp.sem_inc(out_done, 16 * (HALVES + 1))
            sp.sem_inc(fin_in, 32 * HALVES)
            sp.sem_inc(x1_out, 16)
            with sp.Fori(0, HALVES) as s:
                load_half(s, s)
                store_half(s)
            load_half(HALVES % NHALF, HALVES)
            for slot in range(SLOTS):
                load_start(slot, slot, HALVES)
            for slot in range(SLOTS):
                new_state(slot, slot + 1)

            with sp.Fori(0, GROUPS) as g:
                with sp.Fori(0, HALVES) as s:
                    with sp.If(g > 0):
                        last_piece(g, g * HALVES + s)
                    store_half((g + 1) * HALVES + s)
                    load_half(((g + 1) * HALVES + s + 1) % NHALF, (g + 1) * HALVES + s + 1)
                for slot in range(SLOTS):
                    load_start(slot, (g + 1) * SLOTS + slot, HALVES * (g + 2))
                for slot in range(SLOTS):
                    sp.wait_ge(fin_done, SLOTS * g + slot + 1)
                    for q in range(4):
                        sp.dma_start(grid_a_in_dram(yd, g * SLOTS + slot, q),
                                     y[slot][q * C:(q + 1) * C, :].rearrange("c (i j) -> c i j", j=NA)
                                     ).then_inc(y_out[slot], 16)
                    sp.wait_ge(y_out[slot], 64 * g + 64)
                    sp.sem_inc(sp_gate, 1)
                    new_state(slot, SLOTS * (g + 1) + slot + 1)
            for s in range(HALVES):
                last_piece(GROUPS, GROUPS * HALVES + s)
            sp.wait_ge(out_done, 16 * HALVES * (GROUPS + 1) + 16)
            for slot in range(SLOTS):
                sp.wait_ge(y_new[slot], 16 * (GROUPS + 1))
                sp.wait_ge(xa_in[slot], 64 * (GROUPS + 1))
            sp.wait_ge(xs_in, 16 * (HALVES * (GROUPS + 1) + 1))
            sp.wait_ge(x1_out, 16 * HALVES * (GROUPS + 1) + 16)

        @block.gpsimd
        def _(pool):
            def rsqrt(slot, kind, n):
                pool.wait_ge(post_done, NPOST * n + 2)
                nc.gpsimd.tensor_tensor(col(small, slot, kind, RSTD), col(small, slot, kind, VE),
                                        half[:, 0:1], ALU.pow).then_inc(pow_done, 1)

            def zero_rim(slot, lo, rim, own):
                v = hb[slot][:].rearrange("p l (i j) -> p l i j", j=PB)
                for k, (r0, rows) in enumerate(zip(offsets(PARTS_B), PARTS_B)):
                    part, first, last = slice(r0, r0 + rows), slice(0, 1), slice(NB - 1, NB)
                    places = [(0, 64, part, first), (64, 128, part, last)]
                    if k == 0:
                        places += [(0, 32, first, slice(0, NB)), (64, 96, first, slice(0, NB))]
                    if k == NP - 1:
                        places += [(32, 64, last, slice(0, NB)), (96, 128, last, slice(0, NB))]
                    pool.wait_ge(lo_done, lo + k + 1)
                    pool.sem_inc(pool_gate, 1)
                    for m, (p0, p1, ri, rj) in enumerate(places):
                        ins = nc.gpsimd.memset(v[p0:p1, :, ri, rj], 0.0)
                        if m < len(places) - 1:
                            ins.then_inc(pz, 1)
                            own = own + 1
                            pool.wait_ge(pz, own)
                        else:
                            ins.then_inc(rim_zero, 1)
                            pool.wait_ge(rim_zero, rim + k + 1)
                        pool.sem_inc(pool_gate, 1)

            def normalise_half(n):
                pool.wait_ge(s_m0, NHALF_STEPS * (n + 1))
                nc.gpsimd.tensor_tensor(m0[:, 4, 0:CQ], m0[:, 3, CQ:2 * CQ], half[0:H, :], ALU.pow).then_inc(pow0, 1)
                mean = m0[:, 2, 0:CQ].rearrange("p (c o) -> p c o", o=1).broadcast_to([H, CQ, H])
                rstd = m0[:, 4, 0:CQ].rearrange("p (c o) -> p c o", o=1).broadcast_to([H, CQ, H])
                nc.gpsimd.tensor_tensor(xn[:], xs[:], mean, ALU.subtract).then_inc(s_xn, 1)
                pool.wait_ge(s_xn, 2 * n + 1)
                pool.wait_ge(pow0, n + 1)
                nc.gpsimd.tensor_tensor(xn[:], xn[:], rstd, ALU.mult).then_inc(s_xn, 1)

            def last_add(n):
                pool.wait_ge(fin_in, 32 * n + 32)
                o = fin[:, 2, :].rearrange("p (n j r) -> p n r j", j=NA, r=2)
                a = fin[:, 0, :].rearrange("p (n r j) -> p n r j", j=NA, r=2)
                b = fin[:, 1, :].rearrange("p (n r j) -> p n r j", j=NA, r=2)
                nc.gpsimd.tensor_tensor(o, a, b, ALU.add).then_inc(add_done, 1)

            pool.memset(half[:], -0.5).then_inc(pool_set, 1)
            for slot in range(SLOTS):
                pool.memset(ha[slot][:], 0.0).then_inc(pool_set, 1)
            for conv in range(2):
                pool.wait_ge(s_max, conv + 1)
                nc.gpsimd.partition_all_reduce(epsc[:, conv:conv + 1], small[:, 0, conv, 0:1], 128, RMAX
                                               ).then_inc(pool_set, 1)
            pool.wait_ge(pool_set, 1 + SLOTS + 2)
            pool.sem_inc(add_done, HALVES + 1)

            with pool.Fori(0, HALVES) as s:
                normalise_half(s)
            for slot in range(SLOTS):
                rsqrt(slot, IZ, 2 * slot)
                rsqrt(slot, IY, 2 * slot + 1)

            PZ = 8

            def step(g, s, kind):
                lo, rim = parts_before(g, s), 2 * NP * (STEPS * g + s)
                own = 2 * PZ * (STEPS * g + s)
                first = posts_before(g, s)
                for n, (what, slot) in enumerate(POSTS[kind]):
                    rsqrt(slot, what, first + n)
                    if what == Z1:
                        zero_rim(slot, lo + NP * slot, rim + NP * slot, own + PZ * slot)
                    if kind == MID and (what, slot) == (Y, 0):
                        normalise_half(HALVES * (g + 1) + s)
                if kind == MID:
                    with pool.If(g > 0):
                        last_add(g * HALVES + s)

            with pool.Fori(0, GROUPS) as g:
                with pool.Fori(0, HALVES) as s:
                    step(g, s, MID)
                step(g, 4, FOUR)
                step(g, 5, FIVE)
            for s in range(HALVES):
                last_add(GROUPS * HALVES + s)

        @block.scalar
        def _(act):
            def set_bias(conv, t, n):
                src = cbias[:, conv, t:t + 1] if isinstance(t, int) else cbias[:, conv, bass.ds(t, 1)]
                nc.scalar.activation(bias_now[:, conv:conv + 1], src, ACT.Identity).then_inc(bias_set, 1)
                act.wait_ge(bias_set, n + 1)

            def evacuate(slot, conv, k, i, n):
                rows = (TILES1, TILES2)[conv]
                width = (NB, NA)[conv]
                r0, r = offsets(rows)[k], rows[k]
                act.wait_ge(tile_done, n + i + 1)
                nc.scalar.activation(z[slot][:, r0 * width:(r0 + r) * width], cps[i % BANKS][:, 0:r * width],
                                     ACT.Identity, bias=bias_now[:, conv:conv + 1]).then_inc(evac_done, 1)

            def activate(slot, kind, k):
                if kind == Z1:
                    lo = offsets(PARTS_B)[k] * NB
                    n = PARTS_B[k] * NB
                else:
                    lo = offsets(PARTS_A)[k] * NA
                    n = PARTS_A[k] * NA
                src = {Z1: z, Y: y, IY: xa}[kind][slot]
                nc.scalar.activation(z[slot][:, lo:lo + n], src[:, lo:lo + n], ACT.Relu,
                                     bias=col(small, slot, kind, BI), scale=col(small, slot, kind, SC)
                                     ).then_inc(r_done, 1)

            def start_state(slot, n, post):
                act.wait_ge(post_done, post)
                nc.scalar.activation(xa[slot][:], xa[slot][:], ACT.Identity, bias=col(small, slot, IZ, BI),
                                     scale=col(small, slot, IZ, SC), accum_out=isum[:, slot, 0:1]
                                     ).then_inc(y0_done, 1)

            def start_squares(slot, n, adds):
                act.wait_ge(y0_done, n + 1)
                act.wait_ge(isq_done, n + 1)
                act.wait_ge(add_done, adds)
                nc.scalar.activation(fin[:, 0:2, :].rearrange("p a n -> p (a n)"), xa[slot][:], ACT.Square,
                                     accum_out=isum[:, slot, 1:2]).then_inc(isq_done, 1)

            def batch_copy(b, n):
                act.wait_ge(t_done, n + 1)
                nc.scalar.copy(ts[:, b % 2, :, :].rearrange("p c k -> p (c k)"), tps[0:H, 0:4 * H]
                               ).then_inc(ts_done, 1)

            act.sem_inc(isq_done, 1)
            act.sem_inc(ts_done, 1)
            act.wait_ge(set_done, 1)
            with act.Fori(0, HALVES) as s:
                for b in range(NBATCH):
                    batch_copy(b, NBATCH * s + b)
            for slot in range(SLOTS):
                start_state(slot, slot, NPOST * (2 * slot + 1))
                start_squares(slot, slot, HALVES + 1)
            for slot in range(SLOTS):
                act.wait_ge(post_done, NPOST * (2 * slot + 2))
                for k in range(NP):
                    activate(slot, IY, k)
            set_bias(0, 0, 0)
            for k in range(8):
                evacuate(0, 0, k, k, 0)

            def step(g, s, kind):
                n = tiles_before(g, s) - 8
                sq = 2 * NP * (5 * g + s)
                yup = 2 * NP * (STEPS * g + s)

                def posted(what, slot):
                    return NPOST * (posts_before(g, s) + POSTS[kind].index((what, slot)) + 1)

                changes = 1 + 2 * (STEPS * g + s)
                i = 8
                for phase, (slot, other, conv) in enumerate(((1, 0, 0), (0, 1, 1))):
                    if conv == 1:
                        set_bias(1, s, changes)
                    for k in range(len((TILES1, TILES2)[conv])):
                        evacuate(slot, conv, k, i, n)
                        i += 1
                        if k == 1:
                            act.wait_ge(post_done, posted(Z1, other))
                        if 1 <= k <= NP:
                            activate(other, Z1, k - 1)
                        if kind == FOUR and phase == 1 and k == 5:
                            start_state(0, SLOTS * (g + 1), posted(IZ, 0))
                        if kind == FOUR and phase == 1 and k == 6:
                            start_squares(0, SLOTS * (g + 1), HALVES * (g + 1) + 1)
                for phase, (slot, other, conv) in enumerate(((1, 0, 1), (0, 1, 0))):
                    if conv == 0:
                        set_bias(0, s + 1 if kind != FIVE else 0, changes + 1)
                    for k in range(len((TILES1, TILES2)[conv])):
                        evacuate(slot, conv, k, i, n)
                        i += 1
                        if kind != FIVE:
                            if k in (1, 2):
                                for part in (2 * k - 2, 2 * k - 1):
                                    act.wait_ge(yup_done, yup + NP * other + part + 1)
                                    lo, m = offsets(PARTS_A)[part] * NA, PARTS_A[part] * NA
                                    nc.scalar.activation(z[other][:, lo:lo + m], y[other][:, lo:lo + m], ACT.Square,
                                                         accum_out=ysum[:, other, part, 1:2]).then_inc(sq_done, 1)
                            if k == 3:
                                act.wait_ge(post_done, posted(Y, other))
                            if 3 <= k <= 6:
                                activate(other, Y, k - 3)
                        else:
                            if k == 2:
                                act.wait_ge(yup_done, yup + NP * other + NP)
                                act.wait_ge(post_done, posted(Z2, other))
                            if 2 <= k <= 5:
                                activate(other, IY, k - 2)
                            if k == 6:
                                nc.scalar.activation(y[other][:], y[other][:], ACT.Identity,
                                                     bias=last_shift[:, other:other + 1]).then_inc(fin_done, 1)
                        if kind == MID and phase == 1 and 2 <= k < 2 + NBATCH:
                            batch_copy(k - 2, NBATCH * (HALVES * (g + 1) + s) + k - 2)
                        if kind == FOUR and phase == 1 and k == 7:
                            start_state(1, SLOTS * (g + 1) + 1, posted(IZ, 1))
                            start_squares(1, SLOTS * (g + 1) + 1, HALVES * (g + 1) + 1)

            with act.Fori(0, GROUPS) as g:
                with act.Fori(0, HALVES) as s:
                    step(g, s, MID)
                step(g, 4, FOUR)
                step(g, 5, FIVE)

        @block.vector
        def _(dve):
            chain = [0]

            def link(ins):
                chain[0] += 1
                ins.then_inc(s_set, 1)
                dve.wait_ge(s_set, chain[0])

            def setup():
                link(nc.vector.memset(zero[:], 0.0))
                link(nc.vector.memset(ones[:], 1.0))
                dve.wait_ge(setup_in, 16 * 7)
                wsrc = z[0][:, 0:576].rearrange("p (v n) -> p v n", v=2)
                w0v = z[1][:, 0:256].rearrange("p (v n) -> p v n", v=2)
                wi = z[0][:, 1000:1576].rearrange("p (v n) -> p v n", v=2)
                sm = small[:, 1, :, :].rearrange("p a b -> p (a b)")
                ab = sm[:, 0:8]
                link(nc.vector.tensor_scalar(sm[:, 8:16], prm[:], -1.0, None, ALU.mult))
                link(nc.vector.tensor_tensor(ab, prm[:], sm[:, 8:16], ALU.max))
                for conv, (gm, bt) in enumerate(((G1, B1), (G2, B2))):
                    bound, fl = sm[:, 16 + conv:17 + conv], sm[:, 18 + conv:19 + conv]
                    inv = sm[:, 20 + conv:21 + conv]
                    link(nc.vector.tensor_scalar(bound, ab[:, gm:gm + 1], float(H), ab[:, bt:bt + 1],
                                                 ALU.mult, ALU.add))
                    link(nc.vector.tensor_scalar(bound, bound, 1e-18, 1e18, ALU.max, ALU.min))
                    power_of_two(bound, fl, inv)
                    for j in (0, 1):
                        link(nc.vector.tensor_scalar(gb[:, 2 * conv + j:2 * conv + j + 1],
                                                     prm[:, (gm, bt)[j]:(gm, bt)[j] + 1], inv, 2.0 ** 13,
                                                     ALU.mult, ALU.mult))
                    link(nc.vector.tensor_scalar(wi[:, conv, :], wsrc[:, conv, :], fl, 2.0 ** -13,
                                                 ALU.mult, ALU.mult))
                    mx = sm[:, 22:26]
                    link(nc.vector.tensor_reduce(mx[:, 0:1], wi[:, conv, :], AX_X, ALU.max))
                    link(nc.vector.tensor_reduce(mx[:, 1:2], wi[:, conv, :], AX_X, ALU.min))
                    link(nc.vector.tensor_reduce(mx[:, 2:3], w0v[:, conv, :], AX_X, ALU.max))
                    link(nc.vector.tensor_reduce(mx[:, 3:4], w0v[:, conv, :], AX_X, ALU.min))
                    link(nc.vector.tensor_scalar(sm[:, 26:30], mx, -1.0, None, ALU.mult))
                    link(nc.vector.tensor_tensor(mx, mx, sm[:, 26:30], ALU.max))
                    link(nc.vector.tensor_reduce(small[:, 0, conv, 0:1], mx, AX_X, ALU.max))
                    nc.vector.tensor_scalar(sm[:, 30:31], mx[:, 0:1], 1.0, None, ALU.mult).then_inc(s_max, 1)
                    dve.wait_ge(s_max, conv + 1)
                link(nc.vector.tensor_scalar(gb[:, 4:5], prm[:, G3:G3 + 1], DT, None, ALU.mult))
                link(nc.vector.tensor_scalar(gb[:, 5:6], prm[:, B3:B3 + 1], DT, float(STEPS), ALU.mult, ALU.mult))
                dve.wait_ge(pool_set, 1 + SLOTS + 2)
                link(nc.vector.memset(rim_w[:], 0.0))
                for conv, w in enumerate((w1, w2)):
                    s_inv, fl, scale = sm[:, 31:32], sm[:, 32:33], sm[:, 34 + conv:35 + conv]
                    link(nc.vector.tensor_scalar(epsc[:, conv:conv + 1], epsc[:, conv:conv + 1], 1e-18, 1e18,
                                                 ALU.max, ALU.min))
                    power_of_two(epsc[:, conv:conv + 1], fl, s_inv)
                    link(nc.vector.tensor_scalar(scale, s_inv, 2.0 ** 13, None, ALU.mult))
                    link(nc.vector.tensor_scalar(gb[:, 6 + conv:7 + conv], scale, scale, EPS, ALU.mult, ALU.mult))
                    link(nc.vector.tensor_scalar(wi[:, conv, :], wi[:, conv, :], scale, None, ALU.mult))
                    hl = hb[0][:, 0, 0:576].rearrange("p (l k o) -> p l k o", l=2, k=9)
                    v = wi[:, conv, :].rearrange("p (k o) -> p k o", k=9)
                    link(nc.vector.tensor_copy(hl[:, 0], v))
                    link(nc.vector.tensor_tensor(hl[:, 1], v, hl[:, 0], ALU.subtract))
                    link(nc.vector.memset(w[:], 0.0))
                    for q in range(4):
                        ix, iy = q // 2, q % 2
                        for a in range(2):
                            for b in range(2):
                                for qo in range(4):
                                    ox, oy = qo // 2, qo % 2
                                    ky, kx = 2 * a + iy - oy, 2 * b + ix - ox
                                    if 0 <= ky < 3 and 0 <= kx < 3:
                                        last = nc.vector.tensor_copy(
                                            w[q * C:(q + 1) * C, 2 * a + b, :, qo * C:(qo + 1) * C],
                                            hl[q * C:(q + 1) * C, :, 3 * ky + kx, :])
                    link(last)
                    dve.wait_ge(s_rimps, 1)
                    gs = z[0][:, 2000:2128]
                    link(nc.vector.tensor_scalar(gs, cps[conv][:, 0:128], scale, None, ALU.mult))
                    link(nc.vector.tensor_scalar(sm[:, 36:37], cps[2 + conv][:, 0:1], scale, None, ALU.mult))
                    link(nc.vector.tensor_scalar(sm[:, 37:38], prm[:, CB1 + conv:CB1 + conv + 1], scale, None,
                                                 ALU.mult))
                    for k in range(STEPS):
                        t = float(np.float32(DT) * np.float32(k))
                        link(nc.vector.tensor_scalar(cbias[:, conv, k:k + 1], sm[:, 36:37], t, sm[:, 37:38],
                                                     ALU.mult, ALU.add))
                        gk, gh = z[0][:, 2200:2328], hb[0][:, 0, 600:728]
                        link(nc.vector.tensor_scalar(gk, gs, t, None, ALU.mult))
                        link(nc.vector.tensor_copy(gh, gk))
                        link(nc.vector.tensor_copy(rim_w[0:32, conv, k, :], gh[0:32, :]))
                        link(nc.vector.tensor_tensor(rim_w[32:64, conv, k, :], gk[32:64, :], gh[32:64, :],
                                                     ALU.subtract))
                for slot in range(SLOTS):
                    link(nc.vector.tensor_copy(shift[:, slot:slot + 1], gb[:, 5:6]))
                nc.vector.tensor_copy(epsc[:], gb[:, 6:8]).then_inc(set_done, 1)

            def power_of_two(v, fl, inv):
                link(nc.vector.tensor_scalar(fl.bitcast(I32), v.bitcast(I32), 0x7F800000, None, ALU.bitwise_and))
                link(nc.vector.tensor_scalar(inv.bitcast(I32), fl.bitcast(I32), -1.0, float(254 << 23),
                                             ALU.mult, ALU.add))

            def tile_stats(slot, conv, k, n):
                dve.wait_ge(evac_done, n + 1)
                if conv == 1:
                    r0, r = offsets(TILES2)[k], TILES2[k]
                    ins = nc.vector.bn_stats(bn[slot][:, k, :], z[slot][:, r0 * NA:(r0 + r) * NA])
                    if k == 6:
                        ins.then_inc(bn_done, 1)
                    return
                r0, r = offsets(TILES1)[k], TILES1[k]
                a, b = max(r0, 1), min(r0 + r, NB - 1)
                v = z[slot][:, 0:NB * NB].rearrange("p (i j) -> p i j", j=NB)
                nc.vector.bn_stats(bn[slot][:, k, :], v[:, a:b, 1:NB - 1])
                if k == 0:
                    nc.vector.bn_stats(bn[slot][32:64, 8, :], v[32:64, 0, 1:NB])
                    nc.vector.bn_stats(bn[slot][96:128, 8, :], v[96:128, 0, 0:NB - 1])
                if k == 7:
                    nc.vector.bn_stats(bn[slot][0:32, 8, :], v[0:32, NB - 1, 1:NB])
                    nc.vector.bn_stats(bn[slot][64:96, 8, :], v[64:96, NB - 1, 0:NB - 1])
                    nc.vector.bn_stats(bn[slot][64:128, 9, :], v[64:128, 1:NB - 1, 0])
                    nc.vector.bn_stats(bn[slot][0:64, 9, :], v[0:64, 1:NB - 1, NB - 1]).then_inc(bn_done, 1)

            def pre(slot, kind, groups, n):
                src = (bni if kind == IZ else bn)[slot]
                dve.sem_inc(dve_gate, 1)
                nc.vector.bn_aggr(col(small, slot, kind, MEAN, 2), src[:, 0:groups, :].rearrange("p a b -> p (a b)")
                                  ).then_inc(pre_done, 1)
                dve.wait_ge(pre_done, 2 * n + 1)
                nc.vector.scalar_tensor_tensor(out=col(small, slot, kind, E2), in0=col(small, slot, kind, MEAN),
                                               scalar=col(small, slot, kind, MEAN), in1=col(small, slot, kind, E2),
                                               op0=ALU.mult, op1=ALU.add).then_inc(pre_done, 1)

            def post(slot, kind, ev, n, last=False):
                done = NPOST * n
                eps = {Z1: gb[:, 6:7], Z2: gb[:, 7:8]}.get(kind, EPS)
                gamma = {Z1: gb[:, 2:3], Z2: gb[:, 4:5], Y: gb[:, 0:1], IY: gb[:, 0:1], IZ: 1.0}[kind]
                beta = {Z1: gb[:, 3:4], Z2: shift[:, slot:slot + 1], Y: gb[:, 1:2], IY: gb[:, 1:2],
                        IZ: zero[:, 0:1]}[kind]
                bias = col(small, slot, kind, BI)
                if kind == Z2:
                    bias = (last_shift if last else shift)[:, slot:slot + 1]
                dve.wait_ge(stat_done, ev + 1)
                nc.vector.tensor_copy(col(small, slot, kind, MS, 2), sps[:, 0:2]).then_inc(stat_read, 1)
                dve.wait_ge(stat_read, ev + 2)
                nc.vector.scalar_tensor_tensor(out=col(small, slot, kind, VAR), in0=col(small, slot, kind, MS),
                                               scalar=col(small, slot, kind, MS), in1=col(small, slot, kind, ES),
                                               op0=ALU.mult, op1=ALU.subtract, reverse1=True).then_inc(post_done, 1)
                dve.wait_ge(post_done, done + 1)
                nc.vector.tensor_scalar(col(small, slot, kind, VE), col(small, slot, kind, VAR), 0.0, eps,
                                        ALU.max, ALU.add).then_inc(post_done, 1)
                dve.wait_ge(pow_done, n + 1)
                nc.vector.tensor_scalar(col(small, slot, kind, SC), col(small, slot, kind, RSTD), gamma, None,
                                        ALU.mult).then_inc(post_done, 1)
                dve.wait_ge(post_done, done + 3)
                nc.vector.scalar_tensor_tensor(out=bias, in0=col(small, slot, kind, MS),
                                               scalar=col(small, slot, kind, SC), in1=beta,
                                               op0=ALU.mult, op1=ALU.subtract, reverse1=True).then_inc(post_done, 1)
                if kind == Z2:
                    dve.wait_ge(post_done, done + NPOST)

            def split(slot, grid_b, k, n):
                rows = PARTS_B if grid_b else PARTS_A
                width = NB if grid_b else NA
                r0, r = offsets(rows)[k], rows[k]
                src = z[slot][:, r0 * width:(r0 + r) * width].rearrange("p (i j) -> p i j", j=width)
                if grid_b:
                    v = hb[slot][:].rearrange("p l (i j) -> p l i j", j=PB)[:, :, r0:r0 + r, 0:NB]
                else:
                    v = ha[slot][:].rearrange("p l (i j) -> p l i j", j=PADA)[:, :, r0 + 1:r0 + r + 1, 1:NA + 1]
                dve.wait_ge(r_done, n + k + 1)
                nc.vector.tensor_copy(v[:, 0], src).then_inc(hi_done, 1)
                dve.wait_ge(hi_done, n + k + 1)
                nc.vector.tensor_tensor(v[:, 1], src, v[:, 0], ALU.subtract).then_inc(lo_done, 1)

            def euler(slot, k, last):
                lo, m = offsets(PARTS_A)[k] * NA, PARTS_A[k] * NA
                acc = {} if last else {"accum_out": ysum[:, slot, k, 0:1]}
                nc.vector.scalar_tensor_tensor(out=y[slot][:, lo:lo + m], in0=z[slot][:, lo:lo + m],
                                               scalar=col(small, slot, Z2, SC), in1=y[slot][:, lo:lo + m],
                                               op0=ALU.mult, op1=ALU.add, **acc).then_inc(yup_done, 1)

            def start_stats(slot, n):
                dve.wait_ge(xa_in[slot], 64 * n + 64)
                for k in range(7):
                    ins = nc.vector.bn_stats(bni[slot][:, k, :], xa[slot][:, k * 448:(k + 1) * 448])
                ins.then_inc(ibn_done, 1)

            def half_stats(n):
                dve.wait_ge(xs_in, 16 * n + 16)
                for c in range(CQ):
                    ins = nc.vector.bn_stats(bn0[:, c, :], xs[:, c, :])
                b = NHALF_STEPS * n
                ins.then_inc(s_m0, 1)
                dve.wait_ge(s_m0, b + 1)
                me, ve, mo, vo = (bn0[:, :, k] for k in (1, 2, 4, 5))
                nc.vector.tensor_tensor(m0[:, 0, 0:CQ], me, mo, ALU.add).then_inc(s_m0, 1)
                nc.vector.tensor_tensor(m0[:, 1, 0:CQ], ve, vo, ALU.add).then_inc(s_m0, 1)
                nc.vector.tensor_tensor(m0[:, 1, CQ:2 * CQ], me, me, ALU.mult).then_inc(s_m0, 1)
                nc.vector.tensor_tensor(m0[:, 5, 0:CQ], mo, mo, ALU.mult).then_inc(s_m0, 1)
                dve.wait_ge(s_m0, b + 5)
                nc.vector.tensor_tensor(m0[:, 5, CQ:2 * CQ], m0[:, 5, 0:CQ], m0[:, 1, CQ:2 * CQ], ALU.add
                                        ).then_inc(s_m0, 1)
                dve.wait_ge(s_m0, b + 6)
                nc.vector.scalar_tensor_tensor(out=m0[:, 0, CQ:2 * CQ], in0=m0[:, 1, 0:CQ], scalar=2.0 / H,
                                               in1=m0[:, 5, CQ:2 * CQ], op0=ALU.mult, op1=ALU.add).then_inc(s_m0, 1)

            def half_post(n, ev):
                b = NHALF_STEPS * n
                dve.wait_ge(stat_done, ev + 1)
                nc.vector.tensor_copy(m0[:, 2, :], sps[0:H, 0:2 * CQ]).then_inc(stat_read, 1)
                dve.wait_ge(stat_read, ev + 2)
                nc.vector.tensor_tensor(m0[:, 3, 0:CQ], m0[:, 2, 0:CQ], m0[:, 2, 0:CQ], ALU.mult).then_inc(s_m0, 1)
                dve.wait_ge(s_m0, b + 8)
                nc.vector.tensor_tensor(m0[:, 4, CQ:2 * CQ], m0[:, 2, CQ:2 * CQ], m0[:, 3, 0:CQ], ALU.subtract
                                        ).then_inc(s_m0, 1)
                dve.wait_ge(s_m0, b + 9)
                nc.vector.tensor_scalar(m0[:, 3, CQ:2 * CQ], m0[:, 4, CQ:2 * CQ], 0.0, EPS, ALU.max, ALU.add
                                        ).then_inc(s_m0, 1)

            def half_add(b, n):
                dve.wait_ge(xp_done, n + 1)
                xv = xs[:, 4 * b:4 * b + 4, :].rearrange("p c (j r) -> p c r j", r=2)
                nc.vector.tensor_tensor(x1s[:, 4 * b:4 * b + 4], xps[0:H, 0:4 * H].rearrange(
                    "p (c r j) -> p c r j", c=4, r=2), xv, ALU.add).then_inc(x1_done, 1)

            dve.sem_inc(x1_done, 1)
            dve.sem_inc(stat_read, 1)
            setup()
            with dve.Fori(0, HALVES) as s:
                half_stats(s)
                half_post(s, s)
                dve.wait_ge(x1_out, 16 * s + 16)
                for b in range(NBATCH):
                    half_add(b, NBATCH * s + b)
            for slot in range(SLOTS):
                start_stats(slot, 0)
                dve.wait_ge(ibn_done, slot + 1)
                pre(slot, IZ, 7, slot)
                post(slot, IZ, HALVES + 2 * slot, 2 * slot)
                post(slot, IY, HALVES + 2 * slot + 1, 2 * slot + 1)
            for slot in range(SLOTS):
                for k in range(NP):
                    split(slot, False, k, NP * slot)
            for k in range(8):
                tile_stats(0, 0, k, k)

            def step(g, s, kind):
                n = tiles_before(g, s) - 8
                parts = parts_before(g, s)
                bns = 1 + 4 * (STEPS * g + s)
                hn = HALVES * (g + 1) + s

                def pre_of(what, slot, groups):
                    pre(slot, what, groups, pres_before(g, s) + PRES[kind].index((what, slot)))

                def post_of(what, slot, last=False):
                    post(slot, what, stats_before(g, s) + STATS[kind].index((what, slot)),
                         posts_before(g, s) + POSTS[kind].index((what, slot)), last)

                i = 8
                for phase, (slot, other, conv) in enumerate(((1, 0, 0), (0, 1, 1))):
                    dve.wait_ge(bn_done, bns + phase)
                    pre_of(Z1, other, 10)
                    for k in range(len((TILES1, TILES2)[conv])):
                        tile_stats(slot, conv, k, n + i)
                        i += 1
                        if kind == MID and phase == 1 and k == 0:
                            half_post(hn, stats_before(g, s) + STATS[MID].index((X0, 0)))
                        if k == 1:
                            post_of(Z1, other)
                        if 2 <= k <= 5:
                            split(other, True, k - 2, parts + NP * phase)
                        if kind == MID and phase == 0 and k == 5:
                            half_stats(hn)
                        if kind == FOUR and k == 5:
                            start_stats(phase, g + 1)
                            dve.wait_ge(ibn_done, SLOTS * (g + 1) + phase + 1)
                            pre_of(IZ, phase, 7)
                        if kind == FOUR and phase == 0 and k == 7:
                            post_of(IZ, 0)
                        if kind == FIVE and phase == 0 and k == 6:
                            post_of(IY, 1)
                for phase, (slot, other, conv) in enumerate(((1, 0, 1), (0, 1, 0))):
                    dve.wait_ge(bn_done, bns + 2 + phase)
                    pre_of(Z2, other, 7)
                    for k in range(len((TILES1, TILES2)[conv])):
                        tile_stats(slot, conv, k, n + i)
                        i += 1
                        if k == 0:
                            post_of(Z2, other, kind == FIVE)
                            if kind == FIVE:
                                nc.vector.tensor_copy(shift[:, other:other + 1], gb[:, 5:6]).then_inc(shift_set, 1)
                                dve.wait_ge(shift_set, SLOTS * g + phase + 1)
                            dve.wait_ge(y_new[other], 16 * (g + 1))
                        if k in (0, 1):
                            for part in (2 * k, 2 * k + 1):
                                euler(other, part, kind == FIVE)
                        if kind == FOUR and phase == 0 and k == 2:
                            post_of(IZ, 1)
                        if kind != FIVE:
                            if k == 3:
                                post_of(Y, other)
                            if 3 <= k <= 6:
                                split(other, False, k - 3, parts + 2 * NP + NP * phase)
                        elif 2 <= k <= 5:
                            split(other, False, k - 2, parts + 2 * NP + NP * phase)
                        if kind == FOUR and phase == 0 and k == 5:
                            post_of(IY, 0)
                        if kind == MID and phase == 1 and k >= 4:
                            if k == 4:
                                dve.wait_ge(x1_out, 16 * hn + 16)
                            half_add(k - 4, NBATCH * hn + k - 4)

            with dve.Fori(0, GROUPS) as g:
                with dve.Fori(0, HALVES) as s:
                    step(g, s, MID)
                step(g, 4, FOUR)
                step(g, 5, FIVE)

        @block.tensor
        def _(pe):
            def rim_tables():
                pe.wait_ge(setup_in, 16 * 7)
                coef = z[1][:, 256:1280].rearrange("p (v q r) -> p v q r", v=2, q=4)
                w0v = z[1][:, 0:256].rearrange("p (v n) -> p v n", v=2)
                pe.wait_ge(s_set, 2)
                for conv in range(2):
                    for q in range(4):
                        pe.matmul(cps[conv][:, q * C:(q + 1) * C], coef[:, conv, q, :],
                                  w0v[:, conv, q * C:(q + 1) * C], start=True, stop=True)
                    last = pe.matmul(cps[2 + conv][:, 0:1], w0v[:, conv, :], ones[:, 0:1], start=True, stop=True)
                last.then_inc(s_rimps, 1)

            def conv_tile(slot, conv, k, i, t):
                rows = (TILES1, TILES2)[conv]
                r0, r = offsets(rows)[k], rows[k]
                width = (NB, NA)[conv]
                pitch = (PADA, PB)[conv]
                w = (w1, w2)[conv]
                h = (ha, hb)[conv][slot][:].rearrange("p l (i j) -> p l i j", j=pitch)
                ps = cps[i % BANKS][:, 0:r * width].rearrange("p (i j) -> p i j", j=width)
                products = [(tap, wl, hl) for wl, hl in ((0, 0), (0, 1), (1, 0)) for tap in range(4)]

                def product(n):
                    tap, wl, hl = products[n]
                    a, b = tap // 2, tap % 2
                    return pe.matmul(ps, w[:, tap, wl, :], h[:, hl, r0 + a:r0 + a + r, b:b + width],
                                     start=(n == 0), stop=(n == len(products) - 1))

                for m in range(len(products) - 1):
                    product(m)
                rw = rim_w[:, conv, t, :] if isinstance(t, int) else \
                    rim_w[:, conv, bass.ds(t, 1), :].rearrange("p a n -> p (a n)")
                at = (RIM1, RIM2)[conv]
                if k == 0:
                    pe.matmul(ps[:, 0, :], rw, rim_i[:, at:at + width], start=False, stop=False)
                if k == len(rows) - 1:
                    pe.matmul(ps[:, r - 1, :], rw, rim_i[:, at + width:at + 2 * width], start=False, stop=False)
                pe.matmul(ps[:, :, 0:width:width - 1], rw,
                          rim_i[:, RIMC:RIMC + 2 * r].rearrange("p (i j) -> p i j", j=2),
                          start=False, stop=False)
                product(len(products) - 1).then_inc(tile_done, 1)

            def needs(conv, k):
                rows = (TILES1, TILES2)[conv]
                parts = (PARTS_A, PARTS_B)[conv]
                last = offsets(rows)[k] + rows[k] + (0 if conv == 0 else 1)
                last = min(last, sum(parts))
                return next(p + 1 for p in range(NP) if offsets(parts)[p] + parts[p] >= last)

            def tile(slot, conv, k, i, n, t, ready, base):
                if k == 0 or needs(conv, k) > needs(conv, k - 1):
                    pe.wait_ge(ready, base + needs(conv, k))
                if not (isinstance(n, int) and n + i < BANKS):
                    pe.wait_ge(evac_done, n + i - BANKS + 1)
                conv_tile(slot, conv, k, i, t)

            def statistics(slot, kind, ev, wait, value):
                pe.wait_ge(stat_read, ev + 1)
                pe.wait_ge(wait, value)
                if kind in (Z1, Z2, IZ):
                    last = pe.matmul(sps[:, 0:2], mats[:, 0, :], col(small, slot, kind, MEAN, 2),
                                     start=True, stop=True)
                elif kind == IY:
                    last = pe.matmul(sps[:, 0:2], mats[:, 1, :], isum[:, slot, :], start=True, stop=True)
                else:
                    for k in range(NP):
                        last = pe.matmul(sps[:, 0:2], mats[:, 1, :], ysum[:, slot, k, :],
                                         start=(k == 0), stop=(k == NP - 1))
                last.then_inc(stat_done, 1)

            def half_mean(n, ev):
                pe.wait_ge(stat_read, ev + 1)
                pe.wait_ge(s_m0, NHALF_STEPS * n + 7)
                pe.matmul(sps[0:H, 0:2 * CQ], mats[0:H, 2, 0:H], m0[:, 0, :], start=True, stop=True
                          ).then_inc(stat_done, 1)

            def dct_rows(b, n):
                pe.wait_ge(ts_done, n + 1)
                for c in range(4):
                    last = pe.matmul(tps[0:H, c * H:(c + 1) * H], xn[:, 4 * b + c, :], dct[:, 0, :],
                                     start=True, stop=True)
                last.then_inc(t_done, 1)

            def dct_columns(b, n):
                pe.wait_ge(ts_done, n + 2)
                pe.wait_ge(x1_done, n + 1)
                for c in range(4):
                    last = pe.matmul(xps[0:H, c * H:(c + 1) * H], ts[:, b % 2, c, :], dct[:, 1, :],
                                     start=True, stop=True)
                last.then_inc(xp_done, 1)

            def dct_batch(m, hn):
                if m == 0:
                    pe.wait_ge(s_xn, 2 * hn + 2)
                if m < NBATCH:
                    dct_rows(m, NBATCH * hn + m)
                if m > 0:
                    dct_columns(m - 1, NBATCH * hn + m - 1)

            rim_tables()
            with pe.Fori(0, HALVES) as s:
                half_mean(s, s)
                for m in range(NBATCH + 1):
                    dct_batch(m, s)
            for slot in range(SLOTS):
                statistics(slot, IZ, HALVES + 2 * slot, pre_done, 2 * slot + 2)
                statistics(slot, IY, HALVES + 2 * slot + 1, isq_done, slot + 2)
            pe.wait_ge(set_done, 1)
            for k in range(8):
                tile(0, 0, k, k, 0, 0, lo_done, 0)

            def step(g, s, kind):
                n = tiles_before(g, s) - 8
                parts = parts_before(g, s)
                rim = 2 * NP * (STEPS * g + s)
                sq = 2 * NP * (5 * g + s)
                hn = HALVES * (g + 1) + s

                def statistics_of(what, slot):
                    if what in (Z1, Z2, IZ):
                        wait, value = pre_done, 2 * (pres_before(g, s) + PRES[kind].index((what, slot)) + 1)
                    elif what == IY:
                        wait, value = isq_done, SLOTS * (g + 1) + slot + 2
                    else:
                        wait, value = sq_done, sq + NP * (slot + 1)
                    statistics(slot, what, stats_before(g, s) + STATS[kind].index((what, slot)), wait, value)

                i = 8
                for k in range(8):
                    tile(1, 0, k, i, n, s, lo_done, parts - NP)
                    i += 1
                    if k == 1:
                        statistics_of(Z1, 0)
                    if kind == FOUR and k == 6:
                        statistics_of(IZ, 0)
                    if kind == FIVE and k == 4:
                        statistics_of(IY, 1)
                for k in range(7):
                    tile(0, 1, k, i, n, s, rim_zero, rim)
                    i += 1
                    if kind == MID and k == 0:
                        half_mean(hn, stats_before(g, s) + STATS[MID].index((X0, 0)))
                    if k == 1:
                        statistics_of(Z1, 1)
                for k in range(7):
                    tile(1, 1, k, i, n, s, rim_zero, rim + NP)
                    i += 1
                    if k == 0:
                        statistics_of(Z2, 0)
                    if kind == FOUR and k == 1:
                        statistics_of(IZ, 1)
                    if kind != FIVE and k == 3:
                        statistics_of(Y, 0)
                    if kind == FOUR and k == 4:
                        statistics_of(IY, 0)
                for k in range(8):
                    tile(0, 0, k, i, n, s + 1 if kind != FIVE else 0, lo_done, parts + 2 * NP)
                    i += 1
                    if k == 0:
                        statistics_of(Z2, 1)
                    if kind != FIVE and k == 3:
                        statistics_of(Y, 1)
                    if kind == MID and 2 <= k <= 2 + NBATCH:
                        dct_batch(k - 2, hn)

            with pe.Fori(0, GROUPS) as g:
                with pe.Fori(0, HALVES) as s:
                    step(g, s, MID)
                step(g, 4, FOUR)
                step(g, 5, FIVE)


def kernel(**inputs):
    import numpy as _np
    import concourse.bacc as _bacc
    from concourse import mybir as _mybir
    from concourse.bass_utils import run_bass_kernel_spmd as _run

    pre = "L1_conv_"
    x = _np.ascontiguousarray(inputs["x"])
    w = [_np.transpose(inputs[pre + f"conv{k}_w"], (1, 2, 3, 0)) for k in (1, 2)]
    wt = _np.concatenate([_np.tile(v[1:].reshape(C, 9 * C), (4, 1)) for v in w], axis=1)
    w0 = _np.zeros((128, 256), _np.float32)
    w0[0:9] = _np.concatenate([_np.tile(v[0].reshape(9, C), (1, 4)) for v in w], axis=1)
    par = _np.tile(_np.stack([inputs[pre + k] for k in (
        "gn1_w", "gn1_b", "gn2_w", "gn2_b", "gn3_w", "gn3_b", "conv1_b", "conv2_b")], axis=1), (4, 1))
    dct, mats, coef, ind = constants()
    arrays = {"x": x, "wt": wt, "w0": w0, "par": par, "dct": dct, "mats": mats,
              "coef": coef.reshape(128, 1024), "ind": ind}
    nc = _bacc.Bacc("TRN2", target_bir_lowering=False, num_devices=1)
    feed, aps = {}, []
    for name, a in arrays.items():
        a = _np.ascontiguousarray(a)
        feed[f"in_{name}_dram"] = a
        aps.append(nc.dram_tensor(f"in_{name}_dram", a.shape, _mybir.dt.from_np(a.dtype), kind="ExternalInput").ap())
    B = x.shape[0]
    x1d = nc.dram_tensor("x1_dram", (B + SLOTS, C, H, 2, NA), _mybir.dt.float32, kind="Internal").ap()
    yd = nc.dram_tensor("y_dram", (B, C, H, 2, NA), _mybir.dt.float32, kind="Internal").ap()
    out = nc.dram_tensor("out_0_dram", x.shape, _mybir.dt.float32, kind="ExternalOutput").ap()
    build(nc, *aps, x1d, yd, out)
    r = _run(nc, [feed], core_ids=[0])
    return r.results[0]["out_0_dram"]
```

```python
from contextlib import ExitStack

import numpy as np

import concourse.bass as bass
from concourse import mybir

F32 = mybir.dt.float32
F16 = mybir.dt.float16
I32 = mybir.dt.int32
ALU = mybir.AluOpType
ACT = mybir.ActivationFunctionType
AX_X = mybir.AxisListType.X
RMAX = bass.bass_isa.ReduceOp.max

C = 32
H = 112
NA = H // 2
NB = NA + 1
PADA = NA + 2
PB = NB + 1
SLOTS = 2
STEPS = 6
DT = 1.0 / STEPS
EPS = 1e-5
BANKS = 5
TILES1 = [8] + [7] * 7
TILES2 = [8] * 7
PARTS_A = [14] * 4
PARTS_B = [14, 14, 14, 15]
NP = 4
CQ = C // 2
NBATCH = CQ // 4
PIECE = CQ * H * H // 128

Z1, Z2, Y, IZ, IY, X0 = range(6)
MID, FOUR, FIVE = range(3)
STATS = {
    MID: [(Z1, 0), (Z1, 1), (X0, 0), (Z2, 0), (Y, 0), (Z2, 1), (Y, 1)],
    FOUR: [(Z1, 0), (Z1, 1), (Z2, 0), (Y, 0), (Z2, 1), (Y, 1), (IZ, 0)],
    FIVE: [(Z1, 0), (IZ, 1), (Z1, 1), (IY, 0), (Z2, 0), (IY, 1), (Z2, 1)],
}
POSTS = {k: [e for e in v if e[0] != X0] for k, v in STATS.items()}
PRES = {MID: [(Z1, 0), (Z1, 1), (Z2, 0), (Z2, 1)],
        FOUR: [(Z1, 0), (Z1, 1), (Z2, 0), (IZ, 0), (Z2, 1)],
        FIVE: [(Z1, 0), (IZ, 1), (Z1, 1), (Z2, 0), (Z2, 1)]}
START_PLAN = {(0, 5): (0,), (1, 2): (1, 2), (1, 4): (5, 6)}
NPOST = 4
NHALF_STEPS = 10
MEAN, E2, MS, ES, VAR, VE, RSTD, SC, BI = range(9)
G1, B1, G2, B2, G3, B3, CB1, CB2 = range(8)
LO_ROW = 32


def offsets(rows):
    return [sum(rows[:k]) for k in range(len(rows))]


def dct_matrix():
    k = np.arange(H)[:, None].astype(np.float64)
    m = np.arange(H)[None, :].astype(np.float64)
    d = np.cos(np.pi * (2.0 * m + 1.0) * k / (2.0 * H))
    scale = np.full((H, 1), np.sqrt(2.0 / H))
    scale[0, 0] = np.sqrt(1.0 / H)
    return (scale * d).astype(np.float32)


def constants():
    d = dct_matrix()
    dct = np.stack([d.T, d.T.reshape(H, NA, 2).transpose(0, 2, 1).reshape(H, H)], axis=1)
    p = np.arange(128)
    same = (p[:, None] % C == p[None, :] % C).astype(np.float32)
    mats = np.zeros((128, 3, 128), np.float32)
    mats[:, 0] = same / 4
    mats[:, 1] = same / (H * H)
    mats[:, 2] = 0.5 / H
    coef = np.zeros((128, 2, 4, 128), np.float32)
    for conv in range(2):
        for q in range(4):
            rx, ry = q // 2, q % 2
            top, left = (ry == 1, rx == 1) if conv == 0 else (ry == 0, rx == 0)
            for ky in range(3):
                for kx in range(3):
                    row = [0.0] * 8
                    if top and ky == 0:
                        row[0] = -1.0
                        row[1] = float(left and kx == 0)
                        row[2] = float(not left and kx == 2)
                    if not top and ky == 2:
                        row[3] = -1.0
                        row[4] = float(left and kx == 0)
                        row[5] = float(not left and kx == 2)
                    row[6] = -float(left and kx == 0)
                    row[7] = -float(not left and kx == 2)
                    coef[3 * ky + kx, conv, q, 0:8] = row
                    coef[3 * ky + kx, conv, q, LO_ROW:LO_ROW + 8] = row
    ind = np.zeros((128, RIM), np.float16)
    for n, at in ((NB, RIM1), (NA, RIM2)):
        for base in (0, LO_ROW):
            ind[base, at:at + n] = 1
            ind[base + 1, at] = 1
            ind[base + 2, at + n - 1] = 1
            ind[base + 3, at + n:at + 2 * n] = 1
            ind[base + 4, at + n] = 1
            ind[base + 5, at + 2 * n - 1] = 1
    for base in (0, LO_ROW):
        ind[base + 6, RIMC::2] = 1
        ind[base + 7, RIMC + 1::2] = 1
    return dct, mats, coef, ind


RIM1, RIM2, RIMC = 0, 2 * NB, 2 * NB + 2 * NA
RIM = RIMC + 16


def build(nc, x, wt, w0, par, dct_c, mats_c, coef_c, ind_c, x1d, yd, out):
    B = x.shape[0]
    GROUPS = B // SLOTS
    NHALF = 2 * B
    HALVES = 2 * SLOTS

    with ExitStack() as ctx:
        def sb(name, shape, dt=F32):
            return ctx.enter_context(nc.sbuf_tensor(name, shape, dt))

        def pb(name):
            return ctx.enter_context(nc.psum_tensor(name, [128, 512], F32))

        def sem(name):
            return ctx.enter_context(nc.semaphore(name))

        y = [sb(f"y{s}", [128, NA * NA]) for s in range(SLOTS)]
        z = [sb(f"z{s}", [128, (NB + 1) * NB]) for s in range(SLOTS)]
        ha = [sb(f"ha{s}", [128, 2, PADA * PADA], F16) for s in range(SLOTS)]
        hb = [sb(f"hb{s}", [128, 2, (NB + 1) * PB], F16) for s in range(SLOTS)]
        xa = [sb(f"xa{s}", [128, NA * NA]) for s in range(SLOTS)]
        bn = [sb(f"bn{s}", [128, 10, 6]) for s in range(SLOTS)]
        bni = [sb(f"bni{s}", [128, 7, 6]) for s in range(SLOTS)]
        small = sb("small", [128, SLOTS, 5, 9])
        ysum = sb("ysum", [128, SLOTS, NP, 2])
        isum = sb("isum", [128, SLOTS, 2])
        shift = sb("shift", [128, SLOTS])
        xs = sb("xs", [H, CQ, H])
        xn = sb("xn", [H, CQ, H])
        ts = sb("ts", [H, 2, 4, H])
        x1s = sb("x1s", [H, CQ, 2, NA])
        bn0 = sb("bnx", [H, CQ, 6])
        m0 = sb("m0", [H, 6, 2 * CQ])
        fin = sb("fin", [128, 3, PIECE])
        w1 = sb("w1", [128, 4, 2, 128], F16)
        w2 = sb("w2", [128, 4, 2, 128], F16)
        rim_w = sb("rim_w", [128, 2, STEPS, 128], F16)
        rim_i = sb("rim_i", [128, RIM], F16)
        cbias = sb("cbias", [128, 2, STEPS])
        dct = sb("dct", [H, 2, H])
        mats = sb("mats", [128, 3, 128])
        prm = sb("prm", [128, 8])
        gb = sb("gb", [128, 8])
        half = sb("half", [128, CQ])
        epsc = sb("epsc", [128, 2])
        last_shift = sb("last_shift", [128, SLOTS])
        bias_now = sb("bias_now", [128, 2])
        zero = sb("zero", [128, 1])
        ones = sb("ones", [128, 1])

        cps = [pb(f"cps{i}") for i in range(BANKS)]
        sps = pb("sps")
        tps = pb("tps")
        xps = pb("xps")

        setup_in = sem("setup_in")
        s_set = sem("s_set")
        s_max = sem("s_max")
        s_rimps = sem("s_rimps")
        set_done = sem("set_done")
        pool_set = sem("pool_set")
        tile_done = sem("tile_done")
        evac_done = sem("evac_done")
        bn_done = sem("bn_done")
        pre_done = sem("pre_done")
        stat_done = sem("stat_done")
        stat_read = sem("stat_read")
        post_done = sem("post_done")
        pow_done = sem("pow_done")
        r_done = sem("r_done")
        hi_done = sem("hi_done")
        lo_done = sem("lo_done")
        rim_zero = sem("rim_zero")
        sp_gate = sem("sp_gate")
        bias_set = sem("bias_set")
        dve_gate = sem("dve_gate")
        pool_gate = sem("pool_gate")
        pz = sem("pz")
        yup_done = sem("yup_done")
        sq_done = sem("sq_done")
        fin_done = sem("fin_done")
        y_out = [sem(f"y_out{s}") for s in range(SLOTS)]
        y_new = [sem(f"y_new{s}") for s in range(SLOTS)]
        xa_in = [sem(f"xa_in{s}") for s in range(SLOTS)]
        ibn_done = sem("ibn_done")
        y0_done = sem("y0_done")
        isq_done = sem("isq_done")
        shift_set = sem("shift_set")
        xs_in = sem("xs_in")
        s_m0 = sem("s_m0")
        pow0 = sem("pow0")
        s_xn = sem("s_xn")
        t_done = sem("t_done")
        ts_done = sem("ts_done")
        xp_done = sem("xp_done")
        x1_done = sem("x1_done")
        x1_out = sem("x1_out")
        fin_in = sem("fin_in")
        add_done = sem("add_done")
        out_done = sem("out_done")

        def tiles_before(g, s):
            return 8 + 30 * (STEPS * g + s)

        def parts_before(g, s):
            return 2 * NP + 4 * NP * (STEPS * g + s)

        def events_before(table, first, g, s):
            mid, four, five = (len(table[k]) for k in (MID, FOUR, FIVE))
            in_group = 4 * mid + four if isinstance(s, int) and s == 5 else mid * s
            return first + (4 * mid + four + five) * g + in_group

        def stats_before(g, s):
            return events_before(STATS, HALVES + 2 * SLOTS, g, s)

        def posts_before(g, s):
            return events_before(POSTS, 2 * SLOTS, g, s)

        def pres_before(g, s):
            return events_before(PRES, SLOTS, g, s)

        x_half = x.rearrange("b (f c) h w -> (b f) h c w", f=2)
        x1_half = x1d.rearrange("b (f c) h r j -> (b f) h c (r j)", f=2)
        x1_piece = x1d.rearrange("b (f c) h r j -> (b f) (c h r j)", f=2).rearrange("a (p n) -> a p n", p=128)
        y_piece = yd.rearrange("b (f c) h r j -> (b f) (c h r j)", f=2).rearrange("a (p n) -> a p n", p=128)
        out_piece = out.rearrange("b (f c) h w -> (b f) (c h w)", f=2).rearrange("a (p n) -> a p n", p=128)

        def grid_a_in_dram(t, b, q):
            rx, ry = q // 2, q % 2
            v = t.rearrange("b c (i e) r j -> b e r c i j", e=2)
            if isinstance(b, int):
                return v[b, ry, rx]
            return v[bass.ds(b, 1), ry, rx].rearrange("b c i j -> (b c) i j")

        def col(t, slot, kind, k, n=1):
            return t[:, slot, kind, k:k + n]

        block = ctx.enter_context(nc.Block())

        @block.sync
        def _(sp):
            for dst, src in ((prm, par), (mats, mats_c), (rim_i, ind_c)):
                sp.dma_start(dst[:], src).then_inc(setup_in, 16)
            sp.dma_start(z[0][:, 0:2 * 9 * C], wt).then_inc(setup_in, 16)
            sp.dma_start(z[1][:, 0:256], w0).then_inc(setup_in, 16)
            sp.dma_start(z[1][:, 256:256 + 1024], coef_c).then_inc(setup_in, 16)
            sp.dma_start(dct[:], dct_c).then_inc(setup_in, 16)

            def load_half(index, n):
                sp.wait_ge(x1_done, NBATCH * n + 1)
                sp.dma_start(xs[:], x_half[bass.ds(index, 1)].rearrange("a h c w -> (a h) c w")).then_inc(xs_in, 16)

            def store_half(n):
                sp.wait_ge(x1_done, NBATCH * (n + 1) + 1)
                sp.dma_start(x1_half[bass.ds(n, 1)].rearrange("a h c w -> (a h) c w"),
                             x1s[:].rearrange("h c r j -> h c (r j)")).then_inc(x1_out, 16)

            def load_start(slot, b, halves):
                sp.wait_ge(x1_out, 16 * halves + 16)
                for q in range(4):
                    sp.dma_start(xa[slot][q * C:(q + 1) * C, :].rearrange("c (i j) -> c i j", j=NA),
                                 grid_a_in_dram(x1d, b, q)).then_inc(xa_in[slot], 16)

            def new_state(slot, n):
                sp.wait_ge(y0_done, n)
                sp.dma_start(y[slot][:], xa[slot][:]).then_inc(y_new[slot], 16)

            def last_piece(g, n):
                at = bass.ds((n + NHALF - HALVES) % NHALF, 1)
                sp.wait_ge(out_done, 16 * n + 16)
                sp.sem_inc(sp_gate, 1)
                sp.wait_ge(isq_done, SLOTS * (g + 1) + 1)
                sp.dma_start(fin[:, 0, :], x1_piece[at].rearrange("a p n -> (a p) n")).then_inc(fin_in, 16)
                sp.dma_start(fin[:, 1, :], y_piece[at].rearrange("a p n -> (a p) n")).then_inc(fin_in, 16)
                sp.wait_ge(add_done, n + 2)
                sp.dma_start(out_piece[at].rearrange("a p n -> (a p) n"),
                             fin[:, 2, :]).then_inc(out_done, 16)

            sp.sem_inc(out_done, 16 * (HALVES + 1))
            sp.sem_inc(fin_in, 32 * HALVES)
            sp.sem_inc(x1_out, 16)
            with sp.Fori(0, HALVES) as s:
                load_half(s, s)
                store_half(s)
            load_half(HALVES % NHALF, HALVES)
            for slot in range(SLOTS):
                load_start(slot, slot, HALVES)
            for slot in range(SLOTS):
                new_state(slot, slot + 1)

            with sp.Fori(0, GROUPS) as g:
                with sp.Fori(0, HALVES) as s:
                    with sp.If(g > 0):
                        last_piece(g, g * HALVES + s)
                    store_half((g + 1) * HALVES + s)
                    load_half(((g + 1) * HALVES + s + 1) % NHALF, (g + 1) * HALVES + s + 1)
                for slot in range(SLOTS):
                    load_start(slot, (g + 1) * SLOTS + slot, HALVES * (g + 2))
                for slot in range(SLOTS):
                    sp.wait_ge(fin_done, 2 * (SLOTS * g + slot + 1))
                    for q in range(4):
                        sp.dma_start(grid_a_in_dram(yd, g * SLOTS + slot, q),
                                     y[slot][q * C:(q + 1) * C, :].rearrange("c (i j) -> c i j", j=NA)
                                     ).then_inc(y_out[slot], 16)
                    sp.wait_ge(y_out[slot], 64 * g + 64)
                    sp.sem_inc(sp_gate, 1)
                    new_state(slot, SLOTS * (g + 1) + slot + 1)
            for s in range(HALVES):
                last_piece(GROUPS, GROUPS * HALVES + s)
            sp.wait_ge(out_done, 16 * HALVES * (GROUPS + 1) + 16)
            for slot in range(SLOTS):
                sp.wait_ge(y_new[slot], 16 * (GROUPS + 1))
                sp.wait_ge(xa_in[slot], 64 * (GROUPS + 1))
            sp.wait_ge(xs_in, 16 * (HALVES * (GROUPS + 1) + 1))
            sp.wait_ge(x1_out, 16 * HALVES * (GROUPS + 1) + 16)

        @block.gpsimd
        def _(pool):
            def rsqrt(slot, kind, n):
                pool.wait_ge(post_done, NPOST * n + 2)
                nc.gpsimd.tensor_tensor(col(small, slot, kind, RSTD), col(small, slot, kind, VE),
                                        half[:, 0:1], ALU.pow).then_inc(pow_done, 1)

            def zero_rim(slot, lo, rim, own):
                v = hb[slot][:].rearrange("p l (i j) -> p l i j", j=PB)
                for k, (r0, rows) in enumerate(zip(offsets(PARTS_B), PARTS_B)):
                    part, first, last = slice(r0, r0 + rows), slice(0, 1), slice(NB - 1, NB)
                    places = [(0, 64, part, first), (64, 128, part, last)]
                    if k == 0:
                        places += [(0, 32, first, slice(0, NB)), (64, 96, first, slice(0, NB))]
                    if k == NP - 1:
                        places += [(32, 64, last, slice(0, NB)), (96, 128, last, slice(0, NB))]
                    pool.wait_ge(lo_done, lo + k + 1)
                    pool.sem_inc(pool_gate, 1)
                    for m, (p0, p1, ri, rj) in enumerate(places):
                        ins = nc.gpsimd.memset(v[p0:p1, :, ri, rj], 0.0)
                        if m < len(places) - 1:
                            ins.then_inc(pz, 1)
                            own = own + 1
                            pool.wait_ge(pz, own)
                        else:
                            ins.then_inc(rim_zero, 1)
                            pool.wait_ge(rim_zero, rim + k + 1)
                        pool.sem_inc(pool_gate, 1)

            def per_channel(v):
                return v.rearrange("p (c o) -> p c o", o=1).broadcast_to([H, CQ, H])

            def centre_half(n):
                pool.wait_ge(s_m0, NHALF_STEPS * (n + 1))
                nc.gpsimd.tensor_tensor(m0[:, 4, 0:CQ], m0[:, 3, CQ:2 * CQ], half[0:H, :], ALU.pow).then_inc(pow0, 1)
                nc.gpsimd.tensor_tensor(xn[:], xs[:], per_channel(m0[:, 2, 0:CQ]), ALU.subtract).then_inc(s_xn, 1)

            def scale_half(n):
                pool.wait_ge(s_xn, 2 * n + 1)
                pool.wait_ge(pow0, n + 1)
                nc.gpsimd.tensor_tensor(xn[:], xn[:], per_channel(m0[:, 4, 0:CQ]), ALU.mult).then_inc(s_xn, 1)

            def last_add(n):
                pool.wait_ge(fin_in, 32 * n + 32)
                o = fin[:, 2, :].rearrange("p (n j r) -> p n r j", j=NA, r=2)
                a = fin[:, 0, :].rearrange("p (n r j) -> p n r j", j=NA, r=2)
                b = fin[:, 1, :].rearrange("p (n r j) -> p n r j", j=NA, r=2)
                nc.gpsimd.tensor_tensor(o, a, b, ALU.add).then_inc(add_done, 1)

            pool.memset(half[:], -0.5).then_inc(pool_set, 1)
            for slot in range(SLOTS):
                pool.memset(z[slot][:, NB * NB:], 0.0).then_inc(pool_set, 1)
                pool.memset(ha[slot][:], 0.0).then_inc(pool_set, 1)
            for conv in range(2):
                pool.wait_ge(s_max, conv + 1)
                nc.gpsimd.partition_all_reduce(epsc[:, conv:conv + 1], small[:, 0, conv, 0:1], 128, RMAX
                                               ).then_inc(pool_set, 1)
            pool.wait_ge(pool_set, 1 + 2 * SLOTS + 2)
            pool.sem_inc(add_done, HALVES + 1)

            with pool.Fori(0, HALVES) as s:
                centre_half(s)
                scale_half(s)
            for slot in range(SLOTS):
                rsqrt(slot, IZ, 2 * slot)
                rsqrt(slot, IY, 2 * slot + 1)

            PZ = 8

            def step(g, s, kind):
                lo, rim = parts_before(g, s), 2 * NP * (STEPS * g + s)
                own = 2 * PZ * (STEPS * g + s)
                first = posts_before(g, s)
                for n, (what, slot) in enumerate(POSTS[kind]):
                    rsqrt(slot, what, first + n)
                    if what == Z1:
                        zero_rim(slot, lo + NP * slot, rim + NP * slot, own + PZ * slot)
                    if kind == MID and (what, slot) == (Z2, 0):
                        centre_half(HALVES * (g + 1) + s)
                    if kind == MID and (what, slot) == (Y, 0):
                        scale_half(HALVES * (g + 1) + s)
                if kind == MID:
                    with pool.If(g > 0):
                        last_add(g * HALVES + s)

            with pool.Fori(0, GROUPS) as g:
                with pool.Fori(0, HALVES) as s:
                    step(g, s, MID)
                step(g, 4, FOUR)
                step(g, 5, FIVE)
            for s in range(HALVES):
                last_add(GROUPS * HALVES + s)

        @block.scalar
        def _(act):
            def set_bias(conv, t, n):
                src = cbias[:, conv, t:t + 1] if isinstance(t, int) else cbias[:, conv, bass.ds(t, 1)]
                nc.scalar.activation(bias_now[:, conv:conv + 1], src, ACT.Identity).then_inc(bias_set, 1)
                act.wait_ge(bias_set, n + 1)

            def evacuate(slot, conv, k, i, n):
                rows = (TILES1, TILES2)[conv]
                width = (NB, NA)[conv]
                r0, r = offsets(rows)[k], rows[k]
                act.wait_ge(tile_done, n + i + 1)
                nc.scalar.activation(z[slot][:, r0 * width:(r0 + r) * width], cps[i % BANKS][:, 0:r * width],
                                     ACT.Identity, bias=bias_now[:, conv:conv + 1]).then_inc(evac_done, 1)

            def activate(slot, kind, k):
                if kind == Z1:
                    lo = offsets(PARTS_B)[k] * NB
                    n = PARTS_B[k] * NB
                else:
                    lo = offsets(PARTS_A)[k] * NA
                    n = PARTS_A[k] * NA
                src = {Z1: z, Y: y, IY: xa}[kind][slot]
                nc.scalar.activation(z[slot][:, lo:lo + n], src[:, lo:lo + n], ACT.Relu,
                                     bias=col(small, slot, kind, BI), scale=col(small, slot, kind, SC)
                                     ).then_inc(r_done, 1)

            def start_state(slot, n, post):
                act.wait_ge(post_done, post)
                nc.scalar.activation(xa[slot][:], xa[slot][:], ACT.Identity, bias=col(small, slot, IZ, BI),
                                     scale=col(small, slot, IZ, SC), accum_out=isum[:, slot, 0:1]
                                     ).then_inc(y0_done, 1)

            def start_squares(slot, n, adds):
                act.wait_ge(y0_done, n + 1)
                act.wait_ge(isq_done, n + 1)
                act.wait_ge(add_done, adds)
                nc.scalar.activation(fin[:, 0:2, :].rearrange("p a n -> p (a n)"), xa[slot][:], ACT.Square,
                                     accum_out=isum[:, slot, 1:2]).then_inc(isq_done, 1)

            def batch_copy(b, n):
                act.wait_ge(t_done, n + 1)
                nc.scalar.copy(ts[:, b % 2, :, :].rearrange("p c k -> p (c k)"), tps[0:H, 0:4 * H]
                               ).then_inc(ts_done, 1)

            act.sem_inc(isq_done, 1)
            act.sem_inc(ts_done, 1)
            act.wait_ge(set_done, 1)
            with act.Fori(0, HALVES) as s:
                for b in range(NBATCH):
                    batch_copy(b, NBATCH * s + b)
            for slot in range(SLOTS):
                start_state(slot, slot, NPOST * (2 * slot + 1))
                start_squares(slot, slot, HALVES + 1)
            for slot in range(SLOTS):
                act.wait_ge(post_done, NPOST * (2 * slot + 2))
                for k in range(NP):
                    activate(slot, IY, k)
            set_bias(0, 0, 0)
            for k in range(8):
                evacuate(0, 0, k, k, 0)

            def step(g, s, kind):
                n = tiles_before(g, s) - 8
                sq = 2 * NP * (5 * g + s)
                yup = 2 * NP * (STEPS * g + s)

                def posted(what, slot):
                    return NPOST * (posts_before(g, s) + POSTS[kind].index((what, slot)) + 1)

                changes = 1 + 2 * (STEPS * g + s)
                i = 8
                for phase, (slot, other, conv) in enumerate(((1, 0, 0), (0, 1, 1))):
                    if conv == 1:
                        set_bias(1, s, changes)
                    for k in range(len((TILES1, TILES2)[conv])):
                        evacuate(slot, conv, k, i, n)
                        i += 1
                        if k == 1:
                            act.wait_ge(post_done, posted(Z1, other))
                        if 1 <= k <= NP:
                            activate(other, Z1, k - 1)
                        if kind == FIVE and phase == 0 and k == 0:
                            start_state(0, SLOTS * (g + 1), NPOST * (posts_before(g, 4) + POSTS[FOUR].index((IZ, 0)) + 1))
                        if kind == FIVE and phase == 1 and k == 0:
                            start_state(1, SLOTS * (g + 1) + 1, posted(IZ, 1))
                        if kind == FIVE and k == (6, 5)[phase]:
                            start_squares(phase, SLOTS * (g + 1) + phase, HALVES * (g + 1) + 1)
                for phase, (slot, other, conv) in enumerate(((1, 0, 1), (0, 1, 0))):
                    if conv == 0:
                        set_bias(0, s + 1 if kind != FIVE else 0, changes + 1)
                    tiles = len((TILES1, TILES2)[conv])
                    for k in range(tiles):
                        evacuate(slot, conv, k, i, n)
                        i += 1
                        if kind == MID and phase == 1 and 1 <= k <= NBATCH:
                            batch_copy(k - 1, NBATCH * (HALVES * (g + 1) + s) + k - 1)
                        if kind != FIVE and k in (1, 2):
                            for part in (2 * k - 2, 2 * k - 1):
                                act.wait_ge(yup_done, yup + NP * other + part + 1)
                                lo, m = offsets(PARTS_A)[part] * NA, PARTS_A[part] * NA
                                nc.scalar.activation(z[other][:, lo:lo + m], y[other][:, lo:lo + m], ACT.Square,
                                                     accum_out=ysum[:, other, part, 1:2]).then_inc(sq_done, 1)
                        if k == 4:
                            if kind == FIVE:
                                act.wait_ge(yup_done, yup + NP * other + NP)
                                act.wait_ge(post_done, posted(*((IY, 0) if other == 0 else (IY, 1))))
                            else:
                                act.wait_ge(post_done, posted(Y, other))
                        for part in {4: (0, 1), 5: (2,), 6: (3,)}.get(k, ()):
                            activate(other, IY if kind == FIVE else Y, part)
                        if kind == FIVE and k >= tiles - 2:
                            act.wait_ge(post_done, posted(Z2, other))
                            lo, m = (k - tiles + 2) * NA * NA // 2, NA * NA // 2
                            nc.scalar.activation(y[other][:, lo:lo + m], y[other][:, lo:lo + m], ACT.Identity,
                                                 bias=last_shift[:, other:other + 1]).then_inc(fin_done, 1)

            with act.Fori(0, GROUPS) as g:
                with act.Fori(0, HALVES) as s:
                    step(g, s, MID)
                step(g, 4, FOUR)
                step(g, 5, FIVE)

        @block.vector
        def _(dve):
            chain = [0]

            def link(ins):
                chain[0] += 1
                ins.then_inc(s_set, 1)
                dve.wait_ge(s_set, chain[0])

            def setup():
                link(nc.vector.memset(zero[:], 0.0))
                link(nc.vector.memset(ones[:], 1.0))
                dve.wait_ge(setup_in, 16 * 7)
                wsrc = z[0][:, 0:576].rearrange("p (v n) -> p v n", v=2)
                w0v = z[1][:, 0:256].rearrange("p (v n) -> p v n", v=2)
                wi = z[0][:, 1000:1576].rearrange("p (v n) -> p v n", v=2)
                sm = small[:, 1, :, :].rearrange("p a b -> p (a b)")
                ab = sm[:, 0:8]
                link(nc.vector.tensor_scalar(sm[:, 8:16], prm[:], -1.0, None, ALU.mult))
                link(nc.vector.tensor_tensor(ab, prm[:], sm[:, 8:16], ALU.max))
                for conv, (gm, bt) in enumerate(((G1, B1), (G2, B2))):
                    bound, fl = sm[:, 16 + conv:17 + conv], sm[:, 18 + conv:19 + conv]
                    inv = sm[:, 20 + conv:21 + conv]
                    link(nc.vector.tensor_scalar(bound, ab[:, gm:gm + 1], float(H), ab[:, bt:bt + 1],
                                                 ALU.mult, ALU.add))
                    link(nc.vector.tensor_scalar(bound, bound, 1e-18, 1e18, ALU.max, ALU.min))
                    power_of_two(bound, fl, inv)
                    for j in (0, 1):
                        link(nc.vector.tensor_scalar(gb[:, 2 * conv + j:2 * conv + j + 1],
                                                     prm[:, (gm, bt)[j]:(gm, bt)[j] + 1], inv, 2.0 ** 13,
                                                     ALU.mult, ALU.mult))
                    link(nc.vector.tensor_scalar(wi[:, conv, :], wsrc[:, conv, :], fl, 2.0 ** -13,
                                                 ALU.mult, ALU.mult))
                    mx = sm[:, 22:26]
                    link(nc.vector.tensor_reduce(mx[:, 0:1], wi[:, conv, :], AX_X, ALU.max))
                    link(nc.vector.tensor_reduce(mx[:, 1:2], wi[:, conv, :], AX_X, ALU.min))
                    link(nc.vector.tensor_reduce(mx[:, 2:3], w0v[:, conv, :], AX_X, ALU.max))
                    link(nc.vector.tensor_reduce(mx[:, 3:4], w0v[:, conv, :], AX_X, ALU.min))
                    link(nc.vector.tensor_scalar(sm[:, 26:30], mx, -1.0, None, ALU.mult))
                    link(nc.vector.tensor_tensor(mx, mx, sm[:, 26:30], ALU.max))
                    link(nc.vector.tensor_reduce(small[:, 0, conv, 0:1], mx, AX_X, ALU.max))
                    nc.vector.tensor_scalar(sm[:, 30:31], mx[:, 0:1], 1.0, None, ALU.mult).then_inc(s_max, 1)
                    dve.wait_ge(s_max, conv + 1)
                link(nc.vector.tensor_scalar(gb[:, 4:5], prm[:, G3:G3 + 1], DT, None, ALU.mult))
                link(nc.vector.tensor_scalar(gb[:, 5:6], prm[:, B3:B3 + 1], DT, float(STEPS), ALU.mult, ALU.mult))
                dve.wait_ge(pool_set, 1 + 2 * SLOTS + 2)
                link(nc.vector.memset(rim_w[:], 0.0))
                for conv, w in enumerate((w1, w2)):
                    s_inv, fl, scale = sm[:, 31:32], sm[:, 32:33], sm[:, 34 + conv:35 + conv]
                    link(nc.vector.tensor_scalar(epsc[:, conv:conv + 1], epsc[:, conv:conv + 1], 1e-18, 1e18,
                                                 ALU.max, ALU.min))
                    power_of_two(epsc[:, conv:conv + 1], fl, s_inv)
                    link(nc.vector.tensor_scalar(scale, s_inv, 2.0 ** 13, None, ALU.mult))
                    link(nc.vector.tensor_scalar(gb[:, 6 + conv:7 + conv], scale, scale, EPS, ALU.mult, ALU.mult))
                    link(nc.vector.tensor_scalar(wi[:, conv, :], wi[:, conv, :], scale, None, ALU.mult))
                    hl = hb[0][:, 0, 0:576].rearrange("p (l k o) -> p l k o", l=2, k=9)
                    v = wi[:, conv, :].rearrange("p (k o) -> p k o", k=9)
                    link(nc.vector.tensor_copy(hl[:, 0], v))
                    link(nc.vector.tensor_tensor(hl[:, 1], v, hl[:, 0], ALU.subtract))
                    link(nc.vector.memset(w[:], 0.0))
                    for q in range(4):
                        ix, iy = q // 2, q % 2
                        for a in range(2):
                            for b in range(2):
                                for qo in range(4):
                                    ox, oy = qo // 2, qo % 2
                                    ky, kx = 2 * a + iy - oy, 2 * b + ix - ox
                                    if 0 <= ky < 3 and 0 <= kx < 3:
                                        last = nc.vector.tensor_copy(
                                            w[q * C:(q + 1) * C, 2 * a + b, :, qo * C:(qo + 1) * C],
                                            hl[q * C:(q + 1) * C, :, 3 * ky + kx, :])
                    link(last)
                    dve.wait_ge(s_rimps, 1)
                    gs = z[0][:, 2000:2128]
                    link(nc.vector.tensor_scalar(gs, cps[conv][:, 0:128], scale, None, ALU.mult))
                    link(nc.vector.tensor_scalar(sm[:, 36:37], cps[2 + conv][:, 0:1], scale, None, ALU.mult))
                    link(nc.vector.tensor_scalar(sm[:, 37:38], prm[:, CB1 + conv:CB1 + conv + 1], scale, None,
                                                 ALU.mult))
                    for k in range(STEPS):
                        t = float(np.float32(DT) * np.float32(k))
                        link(nc.vector.tensor_scalar(cbias[:, conv, k:k + 1], sm[:, 36:37], t, sm[:, 37:38],
                                                     ALU.mult, ALU.add))
                        gk, gh = z[0][:, 2200:2328], hb[0][:, 0, 600:728]
                        link(nc.vector.tensor_scalar(gk, gs, t, None, ALU.mult))
                        link(nc.vector.tensor_copy(gh, gk))
                        link(nc.vector.tensor_copy(rim_w[0:32, conv, k, :], gh[0:32, :]))
                        link(nc.vector.tensor_tensor(rim_w[32:64, conv, k, :], gk[32:64, :], gh[32:64, :],
                                                     ALU.subtract))
                for slot in range(SLOTS):
                    link(nc.vector.tensor_copy(shift[:, slot:slot + 1], gb[:, 5:6]))
                nc.vector.tensor_copy(epsc[:], gb[:, 6:8]).then_inc(set_done, 1)

            def power_of_two(v, fl, inv):
                link(nc.vector.tensor_scalar(fl.bitcast(I32), v.bitcast(I32), 0x7F800000, None, ALU.bitwise_and))
                link(nc.vector.tensor_scalar(inv.bitcast(I32), fl.bitcast(I32), -1.0, float(254 << 23),
                                             ALU.mult, ALU.add))

            def tile_stats(slot, conv, k, n):
                dve.wait_ge(evac_done, n + 1)
                if conv == 1:
                    r0, r = offsets(TILES2)[k], TILES2[k]
                    ins = nc.vector.bn_stats(bn[slot][:, k, :], z[slot][:, r0 * NA:(r0 + r) * NA])
                    if k == 6:
                        ins.then_inc(bn_done, 1)
                    return
                r0, r = offsets(TILES1)[k], TILES1[k]
                a, b = max(r0, 1), min(r0 + r, NB - 1)
                v = z[slot][:, 0:NB * NB].rearrange("p (i j) -> p i j", j=NB)
                nc.vector.bn_stats(bn[slot][:, k, :], v[:, a:b, 1:NB - 1])
                if k == 0:
                    nc.vector.bn_stats(bn[slot][32:64, 8, :], v[32:64, 0, 1:NB])
                    nc.vector.bn_stats(bn[slot][96:128, 8, :], v[96:128, 0, 0:NB - 1])
                if k == 7:
                    nc.vector.bn_stats(bn[slot][0:32, 8, :], v[0:32, NB - 1, 1:NB])
                    nc.vector.bn_stats(bn[slot][64:96, 8, :], v[64:96, NB - 1, 0:NB - 1])
                    nc.vector.bn_stats(bn[slot][64:128, 9, :], v[64:128, 1:NB - 1, 0])
                    nc.vector.bn_stats(bn[slot][0:64, 9, :], v[0:64, 1:NB - 1, NB - 1]).then_inc(bn_done, 1)

            def pre(slot, kind, groups, n):
                src = (bni if kind == IZ else bn)[slot]
                dve.sem_inc(dve_gate, 1)
                nc.vector.bn_aggr(col(small, slot, kind, MEAN, 2), src[:, 0:groups, :].rearrange("p a b -> p (a b)")
                                  ).then_inc(pre_done, 1)
                dve.wait_ge(pre_done, 2 * n + 1)
                nc.vector.scalar_tensor_tensor(out=col(small, slot, kind, E2), in0=col(small, slot, kind, MEAN),
                                               scalar=col(small, slot, kind, MEAN), in1=col(small, slot, kind, E2),
                                               op0=ALU.mult, op1=ALU.add).then_inc(pre_done, 1)

            def post(slot, kind, ev, n, last=False, meanwhile=None):
                done = NPOST * n
                eps = {Z1: gb[:, 6:7], Z2: gb[:, 7:8]}.get(kind, EPS)
                gamma = {Z1: gb[:, 2:3], Z2: gb[:, 4:5], Y: gb[:, 0:1], IY: gb[:, 0:1], IZ: 1.0}[kind]
                beta = {Z1: gb[:, 3:4], Z2: shift[:, slot:slot + 1], Y: gb[:, 1:2], IY: gb[:, 1:2],
                        IZ: zero[:, 0:1]}[kind]
                bias = col(small, slot, kind, BI)
                if kind == Z2:
                    bias = (last_shift if last else shift)[:, slot:slot + 1]
                dve.wait_ge(stat_done, ev + 1)
                nc.vector.tensor_copy(col(small, slot, kind, MS, 2), sps[:, 0:2]).then_inc(stat_read, 1)
                dve.wait_ge(stat_read, ev + 2)
                nc.vector.scalar_tensor_tensor(out=col(small, slot, kind, VAR), in0=col(small, slot, kind, MS),
                                               scalar=col(small, slot, kind, MS), in1=col(small, slot, kind, ES),
                                               op0=ALU.mult, op1=ALU.subtract, reverse1=True).then_inc(post_done, 1)
                dve.wait_ge(post_done, done + 1)
                nc.vector.tensor_scalar(col(small, slot, kind, VE), col(small, slot, kind, VAR), 0.0, eps,
                                        ALU.max, ALU.add).then_inc(post_done, 1)
                if meanwhile:
                    meanwhile()
                dve.wait_ge(pow_done, n + 1)
                nc.vector.tensor_scalar(col(small, slot, kind, SC), col(small, slot, kind, RSTD), gamma, None,
                                        ALU.mult).then_inc(post_done, 1)
                dve.wait_ge(post_done, done + 3)
                nc.vector.scalar_tensor_tensor(out=bias, in0=col(small, slot, kind, MS),
                                               scalar=col(small, slot, kind, SC), in1=beta,
                                               op0=ALU.mult, op1=ALU.subtract, reverse1=True).then_inc(post_done, 1)
                if kind == Z2:
                    dve.wait_ge(post_done, done + NPOST)

            def split(slot, grid_b, k, n):
                rows = PARTS_B if grid_b else PARTS_A
                width = NB if grid_b else NA
                r0, r = offsets(rows)[k], rows[k]
                if grid_b:
                    r += r % 2
                src = z[slot][:, r0 * width:(r0 + r) * width].rearrange("p (i j) -> p i j", j=width)
                if grid_b:
                    v = hb[slot][:].rearrange("p l (i j) -> p l i j", j=PB)[:, :, r0:r0 + r, 0:NB]
                else:
                    v = ha[slot][:].rearrange("p l (i j) -> p l i j", j=PADA)[:, :, r0 + 1:r0 + r + 1, 1:NA + 1]
                dve.wait_ge(r_done, n + k + 1)
                nc.vector.tensor_copy(v[:, 0], src).then_inc(hi_done, 1)
                dve.wait_ge(hi_done, n + k + 1)
                nc.vector.tensor_tensor(v[:, 1], src, v[:, 0], ALU.subtract).then_inc(lo_done, 1)

            def euler(slot, k, last):
                lo, m = offsets(PARTS_A)[k] * NA, PARTS_A[k] * NA
                acc = {} if last else {"accum_out": ysum[:, slot, k, 0:1]}
                nc.vector.scalar_tensor_tensor(out=y[slot][:, lo:lo + m], in0=z[slot][:, lo:lo + m],
                                               scalar=col(small, slot, Z2, SC), in1=y[slot][:, lo:lo + m],
                                               op0=ALU.mult, op1=ALU.add, **acc).then_inc(yup_done, 1)

            def start_stats(slot, n, tiles):
                if tiles[0] == 0:
                    dve.wait_ge(xa_in[slot], 64 * n + 64)
                for k in tiles:
                    ins = nc.vector.bn_stats(bni[slot][:, k, :], xa[slot][:, k * 448:(k + 1) * 448])
                if tiles[-1] == 6:
                    ins.then_inc(ibn_done, 1)

            def half_stats(n, channels):
                if channels[0] == 0:
                    dve.wait_ge(xs_in, 16 * n + 16)
                for c in channels:
                    ins = nc.vector.bn_stats(bn0[:, c, :], xs[:, c, :])
                if channels[-1] == CQ - 1:
                    ins.then_inc(s_m0, 1)

            def half_pre(n):
                b = NHALF_STEPS * n
                dve.wait_ge(s_m0, b + 1)
                me, ve, mo, vo = (bn0[:, :, k] for k in (1, 2, 4, 5))
                nc.vector.tensor_tensor(m0[:, 0, 0:CQ], me, mo, ALU.add).then_inc(s_m0, 1)
                nc.vector.tensor_tensor(m0[:, 1, 0:CQ], ve, vo, ALU.add).then_inc(s_m0, 1)
                nc.vector.tensor_tensor(m0[:, 1, CQ:2 * CQ], me, me, ALU.mult).then_inc(s_m0, 1)
                nc.vector.tensor_tensor(m0[:, 5, 0:CQ], mo, mo, ALU.mult).then_inc(s_m0, 1)
                dve.wait_ge(s_m0, b + 5)
                nc.vector.tensor_tensor(m0[:, 5, CQ:2 * CQ], m0[:, 5, 0:CQ], m0[:, 1, CQ:2 * CQ], ALU.add
                                        ).then_inc(s_m0, 1)
                dve.wait_ge(s_m0, b + 6)
                nc.vector.scalar_tensor_tensor(out=m0[:, 0, CQ:2 * CQ], in0=m0[:, 1, 0:CQ], scalar=2.0 / H,
                                               in1=m0[:, 5, CQ:2 * CQ], op0=ALU.mult, op1=ALU.add).then_inc(s_m0, 1)

            def half_post(n, ev):
                b = NHALF_STEPS * n
                dve.wait_ge(stat_done, ev + 1)
                nc.vector.tensor_copy(m0[:, 2, :], sps[0:H, 0:2 * CQ]).then_inc(stat_read, 1)
                dve.wait_ge(stat_read, ev + 2)
                nc.vector.tensor_tensor(m0[:, 3, 0:CQ], m0[:, 2, 0:CQ], m0[:, 2, 0:CQ], ALU.mult).then_inc(s_m0, 1)
                dve.wait_ge(s_m0, b + 8)
                nc.vector.tensor_tensor(m0[:, 4, CQ:2 * CQ], m0[:, 2, CQ:2 * CQ], m0[:, 3, 0:CQ], ALU.subtract
                                        ).then_inc(s_m0, 1)
                dve.wait_ge(s_m0, b + 9)
                nc.vector.tensor_scalar(m0[:, 3, CQ:2 * CQ], m0[:, 4, CQ:2 * CQ], 0.0, EPS, ALU.max, ALU.add
                                        ).then_inc(s_m0, 1)

            def half_add(b, n):
                dve.wait_ge(xp_done, n + 1)
                xv = xs[:, 4 * b:4 * b + 4, :].rearrange("p c (j r) -> p c r j", r=2)
                nc.vector.tensor_tensor(x1s[:, 4 * b:4 * b + 4], xps[0:H, 0:4 * H].rearrange(
                    "p (c r j) -> p c r j", c=4, r=2), xv, ALU.add).then_inc(x1_done, 1)

            dve.sem_inc(x1_done, 1)
            dve.sem_inc(stat_read, 1)
            setup()
            with dve.Fori(0, HALVES) as s:
                half_stats(s, range(CQ))
                half_pre(s)
                half_post(s, s)
                dve.wait_ge(x1_out, 16 * s + 16)
                for b in range(NBATCH):
                    half_add(b, NBATCH * s + b)
            for slot in range(SLOTS):
                start_stats(slot, 0, range(7))
                dve.wait_ge(ibn_done, slot + 1)
                pre(slot, IZ, 7, slot)
                post(slot, IZ, HALVES + 2 * slot, 2 * slot)
                post(slot, IY, HALVES + 2 * slot + 1, 2 * slot + 1)
            for slot in range(SLOTS):
                for k in range(NP - slot):
                    split(slot, False, k, NP * slot)
            for k in range(8):
                tile_stats(0, 0, k, k)

            def step(g, s, kind):
                n = tiles_before(g, s) - 8
                parts = parts_before(g, s)
                bns = 1 + 4 * (STEPS * g + s)
                hn = HALVES * (g + 1) + s

                def pre_of(what, slot, groups):
                    pre(slot, what, groups, pres_before(g, s) + PRES[kind].index((what, slot)))

                def post_of(what, slot, last=False, meanwhile=None):
                    post(slot, what, stats_before(g, s) + STATS[kind].index((what, slot)),
                         posts_before(g, s) + POSTS[kind].index((what, slot)), last, meanwhile)

                i = 8
                for phase, (slot, other, conv) in enumerate(((1, 0, 0), (0, 1, 1))):
                    dve.wait_ge(bn_done, bns + phase)
                    pre_of(Z1, other, 10)
                    for k in range(len((TILES1, TILES2)[conv])):
                        tile_stats(slot, conv, k, n + i)
                        i += 1
                        if k == 0:
                            if phase == 0:
                                post_of(Z1, other, meanwhile=lambda: split(1, False, 3, parts - NP))
                            elif kind == MID:
                                post_of(Z1, other, meanwhile=lambda: half_stats(hn, range(12, CQ)))
                            else:
                                post_of(Z1, other)
                        if 1 <= k <= 4:
                            split(other, True, k - 1, parts + NP * phase)
                        if kind == MID and phase == 0 and 2 <= k <= 7:
                            half_stats(hn, range(2 * (k - 2), 2 * (k - 1)))
                        if kind == MID and phase == 1 and k == 2:
                            half_pre(hn)
                        if kind == MID and phase == 1 and k == 6:
                            half_post(hn, stats_before(g, s) + STATS[MID].index((X0, 0)))
                        if kind == FOUR and phase == 1 and k >= 5:
                            start_stats(0, g + 1, range(2 * (k - 5), 2 * (k - 4)))
                        if kind == FIVE and phase == 0 and k == 1:
                            dve.wait_ge(ibn_done, SLOTS * (g + 1) + 2)
                            pre_of(IZ, 1, 7)
                        if kind == FIVE and phase == 0 and k == 7:
                            post_of(IZ, 1)
                        if kind == FIVE and phase == 1 and k == 5:
                            post_of(IY, 0)
                held = 2 if kind == MID else 3
                for phase, (slot, other, conv) in enumerate(((1, 0, 1), (0, 1, 0))):
                    dve.wait_ge(bn_done, bns + 2 + phase)
                    pre_of(Z2, other, 7)
                    state = parts + 2 * NP + NP * phase
                    for k in range(len((TILES1, TILES2)[conv])):
                        if kind == MID and phase == 1 and 3 <= k < 3 + NBATCH:
                            if k == 3:
                                dve.wait_ge(x1_out, 16 * hn + 16)
                            half_add(k - 3, NBATCH * hn + k - 3)
                        tile_stats(slot, conv, k, n + i)
                        i += 1
                        if k == 0:
                            post_of(Z2, other, kind == FIVE,
                                    meanwhile=(lambda: split(0, False, held, state - NP)) if phase == 1 else
                                    (lambda: start_stats(0, g + 1, (4, 5))) if kind == FOUR else None)
                            if kind == FIVE:
                                nc.vector.tensor_copy(shift[:, other:other + 1], gb[:, 5:6]).then_inc(shift_set, 1)
                                dve.wait_ge(shift_set, SLOTS * g + phase + 1)
                            dve.wait_ge(y_new[other], 16 * (g + 1))
                        if phase == 1 and k == 2 and held == 2:
                            split(0, False, 3, state - NP)
                        if k in (0, 1):
                            for part in (2 * k, 2 * k + 1):
                                euler(other, part, kind == FIVE)
                        if kind == FOUR and phase == 0 and k == 4:
                            dve.wait_ge(ibn_done, SLOTS * (g + 1) + 1)
                            pre_of(IZ, 0, 7)
                        if kind == FOUR and (phase, k) in START_PLAN:
                            start_stats(1, g + 1, START_PLAN[phase, k])
                        if kind == FOUR and phase == 1 and k == 6:
                            post_of(IZ, 0, meanwhile=lambda: split(other, False, 2, state))
                            continue
                        if kind == MID and k == 3:
                            post_of(Y, other)
                        if kind == FOUR and k == 3:
                            part = ((6,), (3, 4))[phase]
                            post_of(Y, other, meanwhile=lambda: start_stats(phase, g + 1, part))
                        if kind == FIVE and phase == 0 and k == 4:
                            post_of(IY, 1)
                        if 4 <= k <= (5 + phase if kind == MID else 6):
                            split(other, False, k - 4, state)

            with dve.Fori(0, GROUPS) as g:
                with dve.Fori(0, HALVES) as s:
                    step(g, s, MID)
                step(g, 4, FOUR)
                step(g, 5, FIVE)

        @block.tensor
        def _(pe):
            def rim_tables():
                pe.wait_ge(setup_in, 16 * 7)
                coef = z[1][:, 256:1280].rearrange("p (v q r) -> p v q r", v=2, q=4)
                w0v = z[1][:, 0:256].rearrange("p (v n) -> p v n", v=2)
                pe.wait_ge(s_set, 2)
                for conv in range(2):
                    for q in range(4):
                        pe.matmul(cps[conv][:, q * C:(q + 1) * C], coef[:, conv, q, :],
                                  w0v[:, conv, q * C:(q + 1) * C], start=True, stop=True)
                    last = pe.matmul(cps[2 + conv][:, 0:1], w0v[:, conv, :], ones[:, 0:1], start=True, stop=True)
                last.then_inc(s_rimps, 1)

            def conv_tile(slot, conv, k, i, t, between):
                rows = (TILES1, TILES2)[conv]
                r0, r = offsets(rows)[k], rows[k]
                width = (NB, NA)[conv]
                pitch = (PADA, PB)[conv]
                w = (w1, w2)[conv]
                h = (ha, hb)[conv][slot][:].rearrange("p l (i j) -> p l i j", j=pitch)
                ps = cps[i % BANKS][:, 0:r * width].rearrange("p (i j) -> p i j", j=width)
                products = [(tap, wl, hl) for wl, hl in ((0, 0), (0, 1), (1, 0)) for tap in range(4)]

                def product(n):
                    tap, wl, hl = products[n]
                    a, b = tap // 2, tap % 2
                    return pe.matmul(ps, w[:, tap, wl, :], h[:, hl, r0 + a:r0 + a + r, b:b + width],
                                     start=(n == 0), stop=(n == len(products) - 1))

                for m in range(len(products) - 1):
                    if (k, m) in between:
                        between[k, m]()
                    product(m)
                rw = rim_w[:, conv, t, :] if isinstance(t, int) else \
                    rim_w[:, conv, bass.ds(t, 1), :].rearrange("p a n -> p (a n)")
                at = (RIM1, RIM2)[conv]
                if k == 0:
                    pe.matmul(ps[:, 0, :], rw, rim_i[:, at:at + width], start=False, stop=False)
                if k == len(rows) - 1:
                    pe.matmul(ps[:, r - 1, :], rw, rim_i[:, at + width:at + 2 * width], start=False, stop=False)
                pe.matmul(ps[:, :, 0:width:width - 1], rw,
                          rim_i[:, RIMC:RIMC + 2 * r].rearrange("p (i j) -> p i j", j=2),
                          start=False, stop=False)
                product(len(products) - 1).then_inc(tile_done, 1)

            def needs(conv, k):
                rows = (TILES1, TILES2)[conv]
                parts = (PARTS_A, PARTS_B)[conv]
                last = offsets(rows)[k] + rows[k] + (0 if conv == 0 else 1)
                last = min(last, sum(parts))
                return next(p + 1 for p in range(NP) if offsets(parts)[p] + parts[p] >= last)

            def tile(slot, conv, k, i, n, t, ready, base, between=()):
                if k == 0 or needs(conv, k) > needs(conv, k - 1):
                    pe.wait_ge(ready, base + needs(conv, k))
                if not (isinstance(n, int) and n + i < BANKS):
                    pe.wait_ge(evac_done, n + i - BANKS + 1)
                conv_tile(slot, conv, k, i, t, between)

            def statistics(slot, kind, ev, wait, value):
                pe.wait_ge(stat_read, ev + 1)
                pe.wait_ge(wait, value)
                if kind in (Z1, Z2, IZ):
                    last = pe.matmul(sps[:, 0:2], mats[:, 0, :], col(small, slot, kind, MEAN, 2),
                                     start=True, stop=True)
                elif kind == IY:
                    last = pe.matmul(sps[:, 0:2], mats[:, 1, :], isum[:, slot, :], start=True, stop=True)
                else:
                    for k in range(NP):
                        last = pe.matmul(sps[:, 0:2], mats[:, 1, :], ysum[:, slot, k, :],
                                         start=(k == 0), stop=(k == NP - 1))
                last.then_inc(stat_done, 1)

            def half_mean(n, ev):
                pe.wait_ge(stat_read, ev + 1)
                pe.wait_ge(s_m0, NHALF_STEPS * n + 7)
                pe.matmul(sps[0:H, 0:2 * CQ], mats[0:H, 2, 0:H], m0[:, 0, :], start=True, stop=True
                          ).then_inc(stat_done, 1)

            def dct_rows(b, n):
                pe.wait_ge(ts_done, n + 1)
                for c in range(4):
                    last = pe.matmul(tps[0:H, c * H:(c + 1) * H], xn[:, 4 * b + c, :], dct[:, 0, :],
                                     start=True, stop=True)
                last.then_inc(t_done, 1)

            def dct_columns(b, n):
                pe.wait_ge(ts_done, n + 2)
                pe.wait_ge(x1_done, n + 1)
                for c in range(4):
                    last = pe.matmul(xps[0:H, c * H:(c + 1) * H], ts[:, b % 2, c, :], dct[:, 1, :],
                                     start=True, stop=True)
                last.then_inc(xp_done, 1)

            def rows_of(b, hn):
                if b == 0:
                    pe.wait_ge(s_xn, 2 * hn + 2)
                dct_rows(b, NBATCH * hn + b)

            rim_tables()
            with pe.Fori(0, HALVES) as s:
                half_mean(s, s)
                rows_of(0, s)
                for b in range(NBATCH):
                    if b < NBATCH - 1:
                        rows_of(b + 1, s)
                    dct_columns(b, NBATCH * s + b)
            for slot in range(SLOTS):
                statistics(slot, IZ, HALVES + 2 * slot, pre_done, 2 * slot + 2)
                statistics(slot, IY, HALVES + 2 * slot + 1, isq_done, slot + 2)
            pe.wait_ge(set_done, 1)
            for k in range(8):
                tile(0, 0, k, k, 0, 0, lo_done, 0)

            def step(g, s, kind):
                n = tiles_before(g, s) - 8
                parts = parts_before(g, s)
                rim = 2 * NP * (STEPS * g + s)
                sq = 2 * NP * (5 * g + s)
                hn = HALVES * (g + 1) + s

                def statistics_of(what, slot):
                    if what in (Z1, Z2, IZ):
                        wait, value = pre_done, 2 * (pres_before(g, s) + PRES[kind].index((what, slot)) + 1)
                    elif what == IY:
                        wait, value = isq_done, SLOTS * (g + 1) + slot + 2
                    else:
                        wait, value = sq_done, sq + NP * (slot + 1)
                    statistics(slot, what, stats_before(g, s) + STATS[kind].index((what, slot)), wait, value)

                def among(*places):
                    return {(k, m): (lambda e=event: statistics_of(*e)) for k, m, event in places}

                i = 8
                between = among((2, 6 if kind == FIVE else 0, (Z1, 0)))
                if kind == FIVE:
                    between.update(among((7, 0, (IZ, 1))))
                for k in range(8):
                    tile(1, 0, k, i, n, s, lo_done, parts - NP, between)
                    i += 1
                between = among((2, 0, (Z1, 1)) if kind == FIVE else (1, 9, (Z1, 1)))
                if kind == MID:
                    between[5, 6] = lambda: half_mean(hn, stats_before(g, s) + STATS[MID].index((X0, 0)))
                if kind == FIVE:
                    between.update(among((5, 0, (IY, 0))))
                for k in range(7):
                    tile(0, 1, k, i, n, s, rim_zero, rim, between)
                    i += 1
                between = among((1, 9 if kind == FIVE else 3, (Z2, 0)))
                if kind != FIVE:
                    between.update(among((4, 9, (Y, 0))))
                else:
                    between.update(among((4, 0, (IY, 1))))
                for k in range(7):
                    tile(1, 1, k, i, n, s, rim_zero, rim + NP, between)
                    i += 1
                between = among((1, 3 if kind == MID else 9, (Z2, 1)))
                if kind != FIVE:
                    between.update(among((4, 2, (Y, 1)) if kind == MID else (5, 5, (Y, 1))))
                if kind == FOUR:
                    between.update(among((6, 3, (IZ, 0))))
                if kind == MID:
                    for b in range(NBATCH):
                        between[2 + b, 0] = lambda b=b: rows_of(b, hn)
                        between[3 + b, 9] = lambda b=b: dct_columns(b, NBATCH * hn + b)
                for k in range(8):
                    tile(0, 0, k, i, n, s + 1 if kind != FIVE else 0, lo_done, parts + 2 * NP, between)
                    i += 1

            with pe.Fori(0, GROUPS) as g:
                with pe.Fori(0, HALVES) as s:
                    step(g, s, MID)
                step(g, 4, FOUR)
                step(g, 5, FIVE)


def kernel(**inputs):
    import numpy as _np
    import concourse.bacc as _bacc
    from concourse import mybir as _mybir
    from concourse.bass_utils import run_bass_kernel_spmd as _run

    pre = "L1_conv_"
    x = _np.ascontiguousarray(inputs["x"])
    w = [_np.transpose(inputs[pre + f"conv{k}_w"], (1, 2, 3, 0)) for k in (1, 2)]
    wt = _np.concatenate([_np.tile(v[1:].reshape(C, 9 * C), (4, 1)) for v in w], axis=1)
    w0 = _np.zeros((128, 256), _np.float32)
    w0[0:9] = _np.concatenate([_np.tile(v[0].reshape(9, C), (1, 4)) for v in w], axis=1)
    par = _np.tile(_np.stack([inputs[pre + k] for k in (
        "gn1_w", "gn1_b", "gn2_w", "gn2_b", "gn3_w", "gn3_b", "conv1_b", "conv2_b")], axis=1), (4, 1))
    dct, mats, coef, ind = constants()
    arrays = {"x": x, "wt": wt, "w0": w0, "par": par, "dct": dct, "mats": mats,
              "coef": coef.reshape(128, 1024), "ind": ind}
    nc = _bacc.Bacc("TRN2", target_bir_lowering=False, num_devices=1)
    feed, aps = {}, []
    for name, a in arrays.items():
        a = _np.ascontiguousarray(a)
        feed[f"in_{name}_dram"] = a
        aps.append(nc.dram_tensor(f"in_{name}_dram", a.shape, _mybir.dt.from_np(a.dtype), kind="ExternalInput").ap())
    B = x.shape[0]
    x1d = nc.dram_tensor("x1_dram", (B + SLOTS, C, H, 2, NA), _mybir.dt.float32, kind="Internal").ap()
    yd = nc.dram_tensor("y_dram", (B, C, H, 2, NA), _mybir.dt.float32, kind="Internal").ap()
    out = nc.dram_tensor("out_0_dram", x.shape, _mybir.dt.float32, kind="ExternalOutput").ap()
    build(nc, *aps, x1d, yd, out)
    r = _run(nc, [feed], core_ids=[0])
    return r.results[0]["out_0_dram"]
```

```python
from contextlib import ExitStack

import numpy as np

import concourse.bass as bass
from concourse import mybir

F32 = mybir.dt.float32
F16 = mybir.dt.float16
I32 = mybir.dt.int32
ALU = mybir.AluOpType
ACT = mybir.ActivationFunctionType
AX_X = mybir.AxisListType.X
RMAX = bass.bass_isa.ReduceOp.max

C = 32
H = 112
NA = H // 2
NB = NA + 1
PADA = NA + 2
PB = NB + 1
SLOTS = 2
STEPS = 6
DT = 1.0 / STEPS
EPS = 1e-5
BANKS = 5
TILES1 = [8] + [7] * 7
TILES2 = [8] * 7
PARTS_A = [14] * 4
PARTS_B = [14, 14, 14, 15]
NP = 4
CQ = C // 2
NBATCH = CQ // 4
PIECE = CQ * H * H // 128

Z1, Z2, Y, IZ, IY, X0 = range(6)
MID, FOUR, FIVE, LAST_MID, LAST = range(5)
STATS = {
    MID: [(Z1, 0), (Z1, 1), (X0, 0), (Z2, 0), (Y, 0), (Z2, 1), (Y, 1)],
    FOUR: [(Z1, 0), (Z1, 1), (Z2, 0), (Y, 0), (Z2, 1), (Y, 1), (IZ, 0)],
    FIVE: [(Z1, 0), (IZ, 1), (Z1, 1), (IY, 0), (Z2, 0), (IY, 1), (Z2, 1)],
    LAST_MID: [(Z1, 0), (Z1, 1), (Z2, 0), (Y, 0), (Z2, 1), (Y, 1)],
    LAST: [(Z1, 0), (Z1, 1), (Z2, 0), (Z2, 1)],
}
POSTS = {k: [e for e in v if e[0] != X0] for k, v in STATS.items()}
PRES = {MID: [(Z1, 0), (Z1, 1), (Z2, 0), (Z2, 1)],
        FOUR: [(Z1, 0), (Z1, 1), (Z2, 0), (IZ, 0), (Z2, 1)],
        FIVE: [(Z1, 0), (IZ, 1), (Z1, 1), (Z2, 0), (Z2, 1)],
        LAST_MID: [(Z1, 0), (Z1, 1), (Z2, 0), (Z2, 1)],
        LAST: [(Z1, 0), (Z1, 1), (Z2, 0), (Z2, 1)]}
START_PLAN = {(0, 1): (0,), (0, 2): (1,), (0, 5): (2,), (1, 2): (3,), (1, 4): (6,)}
NPOST = 4
NHALF_STEPS = 10
MEAN, E2, MS, ES, VAR, VE, RSTD, SC, BI = range(9)
G1, B1, G2, B2, G3, B3, CB1, CB2 = range(8)
LO_ROW = 32


def offsets(rows):
    return [sum(rows[:k]) for k in range(len(rows))]


def dct_matrix():
    k = np.arange(H)[:, None].astype(np.float64)
    m = np.arange(H)[None, :].astype(np.float64)
    d = np.cos(np.pi * (2.0 * m + 1.0) * k / (2.0 * H))
    scale = np.full((H, 1), np.sqrt(2.0 / H))
    scale[0, 0] = np.sqrt(1.0 / H)
    return (scale * d).astype(np.float32)


def constants():
    d = dct_matrix()
    dct = np.stack([d.T, d.T.reshape(H, NA, 2).transpose(0, 2, 1).reshape(H, H)], axis=1)
    p = np.arange(128)
    same = (p[:, None] % C == p[None, :] % C).astype(np.float32)
    mats = np.zeros((128, 3, 128), np.float32)
    mats[:, 0] = same / 4
    mats[:, 1] = same / (H * H)
    mats[:, 2] = 0.5 / H
    coef = np.zeros((128, 2, 4, 128), np.float32)
    for conv in range(2):
        for q in range(4):
            rx, ry = q // 2, q % 2
            top, left = (ry == 1, rx == 1) if conv == 0 else (ry == 0, rx == 0)
            for ky in range(3):
                for kx in range(3):
                    row = [0.0] * 8
                    if top and ky == 0:
                        row[0] = -1.0
                        row[1] = float(left and kx == 0)
                        row[2] = float(not left and kx == 2)
                    if not top and ky == 2:
                        row[3] = -1.0
                        row[4] = float(left and kx == 0)
                        row[5] = float(not left and kx == 2)
                    row[6] = -float(left and kx == 0)
                    row[7] = -float(not left and kx == 2)
                    coef[3 * ky + kx, conv, q, 0:8] = row
                    coef[3 * ky + kx, conv, q, LO_ROW:LO_ROW + 8] = row
    ind = np.zeros((128, RIM), np.float16)
    for n, at in ((NB, RIM1), (NA, RIM2)):
        for base in (0, LO_ROW):
            ind[base, at:at + n] = 1
            ind[base + 1, at] = 1
            ind[base + 2, at + n - 1] = 1
            ind[base + 3, at + n:at + 2 * n] = 1
            ind[base + 4, at + n] = 1
            ind[base + 5, at + 2 * n - 1] = 1
    for base in (0, LO_ROW):
        ind[base + 6, RIMC::2] = 1
        ind[base + 7, RIMC + 1::2] = 1
    return dct, mats, coef, ind


RIM1, RIM2, RIMC = 0, 2 * NB, 2 * NB + 2 * NA
RIM = RIMC + 16


def build(nc, x, wt, w0, par, dct_c, mats_c, coef_c, ind_c, x1d, yd, out):
    B = x.shape[0]
    GROUPS = B // SLOTS
    NHALF = 2 * B
    HALVES = 2 * SLOTS

    with ExitStack() as ctx:
        def sb(name, shape, dt=F32):
            return ctx.enter_context(nc.sbuf_tensor(name, shape, dt))

        def pb(name):
            return ctx.enter_context(nc.psum_tensor(name, [128, 512], F32))

        def sem(name):
            return ctx.enter_context(nc.semaphore(name))

        y = [sb(f"y{s}", [128, NA * NA]) for s in range(SLOTS)]
        z = [sb(f"z{s}", [128, (NB + 1) * NB]) for s in range(SLOTS)]
        ha = [sb(f"ha{s}", [128, 2, PADA * PADA], F16) for s in range(SLOTS)]
        hb = [sb(f"hb{s}", [128, 2, (NB + 1) * PB], F16) for s in range(SLOTS)]
        xa = [sb(f"xa{s}", [128, NA * NA]) for s in range(SLOTS)]
        bn = [sb(f"bnt{s}", [128, 10, 6]) for s in range(SLOTS)]
        bni = [sb(f"bni{s}", [128, 7, 6]) for s in range(SLOTS)]
        small = sb("small", [128, SLOTS, 5, 9])
        ysum = sb("ysum", [128, SLOTS, NP, 2])
        isum = sb("isum", [128, SLOTS, 2])
        shift = sb("shift", [128, SLOTS])
        xs = sb("xs", [H, CQ, H])
        xn = sb("xn", [H, CQ, H])
        ts = sb("ts", [H, 2, 4, H])
        x1s = sb("x1s", [H, CQ, 2, NA])
        bn0 = sb("bn0", [H, CQ, 6])
        m0 = sb("m0", [H, 6, 2 * CQ])
        bn0b = sb("bn0b", [H, CQ, 6])
        m0b = sb("m0b", [H, 6, 2 * CQ])
        fin = sb("fin", [128, 3, PIECE])
        xsb = fin[:].rearrange("p a n -> p (a n)")[0:H, 0:CQ * H].rearrange("h (c w) -> h c w", c=CQ)
        xnb = fin[:].rearrange("p a n -> p (a n)")[0:H, CQ * H:2 * CQ * H].rearrange("h (c w) -> h c w", c=CQ)
        x1b = y[1][0:H, 0:CQ * H].rearrange("h (c r j) -> h c r j", c=CQ, r=2)
        FIRST, SECOND = (xs[:], xn[:], x1s[:], bn0[:], m0[:]), (xsb, xnb, x1b, bn0b[:], m0b[:])
        w1 = sb("w1", [128, 4, 2, 128], F16)
        w2 = sb("w2", [128, 4, 2, 128], F16)
        rim_w = sb("rim_w", [128, 2, STEPS, 128], F16)
        rim_i = sb("rim_i", [128, RIM], F16)
        cbias = sb("cbias", [128, 2, STEPS])
        dct = sb("dct", [H, 2, H])
        mats = sb("mats", [128, 3, 128])
        prm = sb("prm", [128, 8])
        gb = sb("gb", [128, 8])
        half = sb("half", [128, CQ])
        epsc = sb("epsc", [128, 2])
        last_shift = sb("last_shift", [128, SLOTS])
        bias_now = sb("bias_now", [128, 2])
        zero = sb("zero", [128, 1])
        ones = sb("ones", [128, 1])

        cps = [pb(f"cps{i}") for i in range(BANKS)]
        sps = pb("sps")
        tps = pb("tps")
        xps = pb("xps")

        setup_in = sem("setup_in")
        s_set = sem("s_set")
        s_max = sem("s_max")
        s_rimps = sem("s_rimps")
        set_done = sem("set_done")
        pool_set = sem("pool_set")
        tile_done = sem("tile_done")
        evac_done = sem("evac_done")
        bn_done = sem("bn_done")
        pre_done = sem("pre_done")
        stat_done = sem("stat_done")
        stat_read = sem("stat_read")
        post_done = sem("post_done")
        pow_done = sem("pow_done")
        r_done = sem("r_done")
        hi_done = sem("hi_done")
        lo_done = sem("lo_done")
        rim_zero = sem("rim_zero")
        sp_gate = sem("sp_gate")
        bias_set = sem("bias_set")
        dve_gate = sem("dve_gate")
        pool_gate = sem("pool_gate")
        pz = sem("pz")
        yup_done = sem("yup_done")
        sq_done = sem("sq_done")
        fin_done = sem("fin_done")
        y_out = [sem(f"y_out{s}") for s in range(SLOTS)]
        y_new = [sem(f"y_new{s}") for s in range(SLOTS)]
        xa_in = [sem(f"xa_in{s}") for s in range(SLOTS)]
        ibn_done = sem("ibn_done")
        y0_done = sem("y0_done")
        isq_done = sem("isq_done")
        shift_set = sem("shift_set")
        xs_in = sem("xs_in")
        xsb_in = sem("xsb_in")
        s_m0 = sem("s_m0")
        pow0 = sem("pow0")
        s_xn = sem("s_xn")
        s_xnb = sem("s_xnb")
        t_done = sem("t_done")
        ts_done = sem("ts_done")
        xp_done = sem("xp_done")
        x1_done = sem("x1_done")
        x1_out = sem("x1_out")
        x1b_out = sem("x1b_out")
        fin_in = sem("fin_in")
        add_done = sem("add_done")
        out_done = sem("out_done")
        x1_tail = sem("x1_tail")
        y_tail = [sem(f"y_tail{s}") for s in range(SLOTS)]
        add_tail = [sem(f"add_tail{s}") for s in range(SLOTS)]
        out_tail = sem("out_tail")

        def tiles_before(g, s):
            return 8 + 30 * (STEPS * g + s)

        def parts_before(g, s):
            return 2 * NP + 4 * NP * (STEPS * g + s)

        def events_before(table, first, g, s, kind):
            mid, four, five = (len(table[k]) for k in (MID, FOUR, FIVE))
            if kind in (LAST_MID, LAST):
                in_group = len(table[LAST_MID]) * s
            else:
                in_group = 4 * mid + four if kind == FIVE else mid * s
            return first + (4 * mid + four + five) * g + in_group

        def stats_before(g, s, kind):
            return events_before(STATS, HALVES + 2 * SLOTS, g, s, kind)

        def posts_before(g, s, kind):
            return events_before(POSTS, 2 * SLOTS, g, s, kind)

        def pres_before(g, s, kind):
            return events_before(PRES, SLOTS, g, s, kind)

        def first_place(n):
            return n - SLOTS

        def tail_sum(engine, slot, k):
            def piece(t, at=0):
                return t[:, at:at + PIECE]
            o = piece(z[slot], k * PIECE).rearrange("p (n j r) -> p n r j", j=NA, r=2)
            a = piece(xa[slot], k * PIECE).rearrange("p (n r j) -> p n r j", j=NA, r=2)
            b = tail_y(slot, k).rearrange("p (n r j) -> p n r j", j=NA, r=2)
            engine.tensor_tensor(o, a, b, ALU.add).then_inc(add_tail[slot], 1)

        def tail_y(slot, k):
            return fin[:, k, :] if slot == 0 else y[0][:, k * PIECE:(k + 1) * PIECE]

        x_half = x.rearrange("b (f c) h w -> (b f) h c w", f=2)
        x1_half = x1d.rearrange("b (f c) h r j -> (b f) h c (r j)", f=2)
        x1_piece = x1d.rearrange("b (f c) h r j -> (b f) (c h r j)", f=2).rearrange("a (p n) -> a p n", p=128)
        y_piece = yd.rearrange("b (f c) h r j -> (b f) (c h r j)", f=2).rearrange("a (p n) -> a p n", p=128)
        out_piece = out.rearrange("b (f c) h w -> (b f) (c h w)", f=2).rearrange("a (p n) -> a p n", p=128)

        def grid_a_in_dram(t, b, q):
            rx, ry = q // 2, q % 2
            v = t.rearrange("b c (i e) r j -> b e r c i j", e=2)
            if isinstance(b, int):
                return v[b, ry, rx]
            return v[bass.ds(b, 1), ry, rx].rearrange("b c i j -> (b c) i j")

        def col(t, slot, kind, k, n=1):
            return t[:, slot, kind, k:k + n]

        block = ctx.enter_context(nc.Block())

        @block.sync
        def _(sp):
            def setup_loads():
                for dst, src in ((prm, par), (mats, mats_c), (rim_i, ind_c)):
                    sp.dma_start(dst[:], src).then_inc(setup_in, 16)
                sp.dma_start(z[0][:, 0:2 * 9 * C], wt).then_inc(setup_in, 16)
                sp.dma_start(z[1][:, 0:256], w0).then_inc(setup_in, 16)
                sp.dma_start(z[1][:, 256:256 + 1024], coef_c).then_inc(setup_in, 16)
                sp.dma_start(dct[:], dct_c).then_inc(setup_in, 16)

            def load_half(index, n):
                sp.wait_ge(x1_done, NBATCH * n + 1)
                sp.dma_start(xs[:], x_half[bass.ds(index, 1)].rearrange("a h c w -> (a h) c w")).then_inc(xs_in, 16)

            def load_first(image, k):
                dst, arrived = ((xs[:], xs_in), (xsb, xsb_in))[k]
                sp.dma_start(dst, x_half[2 * image + k]).then_inc(arrived, 16)

            def store_first(image, k):
                src, left = ((x1s[:], x1_out), (x1b, x1b_out))[k]
                sp.dma_start(x1_half[2 * image + k], src.rearrange("h c r j -> h c (r j)")).then_inc(left, 16)

            def store_half(n):
                sp.wait_ge(x1_done, NBATCH * (n + 1) + 1)
                sp.dma_start(x1_half[bass.ds(n, 1)].rearrange("a h c w -> (a h) c w"),
                             x1s[:].rearrange("h c r j -> h c (r j)")).then_inc(x1_out, 16)

            def load_start(slot, b):
                for q in range(4):
                    sp.dma_start(xa[slot][q * C:(q + 1) * C, :].rearrange("c (i j) -> c i j", j=NA),
                                 grid_a_in_dram(x1d, b, q)).then_inc(xa_in[slot], 16)

            def new_state(slot, n):
                sp.wait_ge(y0_done, n)
                sp.dma_start(y[slot][:], xa[slot][:]).then_inc(y_new[slot], 16)

            def last_piece(g, n):
                at = bass.ds((n + NHALF - HALVES) % NHALF, 1)
                sp.wait_ge(out_done, 16 * n + 16)
                sp.sem_inc(sp_gate, 1)
                sp.wait_ge(isq_done, SLOTS * (g + 1) + 1)
                sp.dma_start(fin[:, 0, :], x1_piece[at].rearrange("a p n -> (a p) n")).then_inc(fin_in, 16)
                sp.dma_start(fin[:, 1, :], y_piece[at].rearrange("a p n -> (a p) n")).then_inc(fin_in, 16)
                sp.wait_ge(add_done, n + 2)
                sp.dma_start(out_piece[at].rearrange("a p n -> (a p) n"),
                             fin[:, 2, :]).then_inc(out_done, 16)

            sp.sem_inc(out_done, 16 * (HALVES + 1))
            sp.sem_inc(fin_in, 32 * HALVES)
            sp.sem_inc(x1_out, 16)
            load_first(0, 0)
            load_first(0, 1)
            setup_loads()
            for image in range(SLOTS):
                for k in range(2):
                    sp.wait_ge(x1_done, NBATCH * (2 * image + k + 1) + 1)
                    if image + 1 < SLOTS:
                        load_first(image + 1, k)
                    store_first(image, k)
                sp.wait_ge(x1_out, 16 * image + 32)
                sp.wait_ge(x1b_out, 16 * image + 16)
                load_start(image, image)
            load_half(HALVES % NHALF, HALVES)
            for slot in range(SLOTS):
                new_state(slot, slot + 1)

            def store_state(g, slot):
                sp.wait_ge(fin_done, 2 * (SLOTS * g + slot + 1))
                for q in range(4):
                    sp.dma_start(grid_a_in_dram(yd, g * SLOTS + slot, q),
                                 y[slot][q * C:(q + 1) * C, :].rearrange("c (i j) -> c i j", j=NA)
                                 ).then_inc(y_out[slot], 16)

            LG = GROUPS - 1
            with sp.Fori(0, LG) as g:
                with sp.Fori(0, HALVES) as s:
                    with sp.If(g > 0):
                        last_piece(g, g * HALVES + s)
                    store_half((g + 1) * HALVES + s)
                    load_half(((g + 1) * HALVES + s + 1) % NHALF, (g + 1) * HALVES + s + 1)
                sp.wait_ge(x1_out, 16 * first_place(HALVES * (g + 2)) + 16)
                for slot in range(SLOTS):
                    load_start(slot, (g + 1) * SLOTS + slot)
                for slot in range(SLOTS):
                    store_state(g, slot)
                    sp.wait_ge(y_out[slot], 64 * g + 64)
                    sp.sem_inc(sp_gate, 1)
                    new_state(slot, SLOTS * (g + 1) + slot + 1)
            with sp.Fori(0, HALVES) as s:
                last_piece(LG, LG * HALVES + s)
            sp.wait_ge(sq_done, 2 * NP * 5 * LG + 1)
            for slot in range(SLOTS):
                sp.wait_ge(y_new[slot], 16 * GROUPS)
                for k in range(2):
                    sp.dma_start(xa[slot][:, k * PIECE:(k + 1) * PIECE], x1_piece[LG * HALVES + 2 * slot + k]
                                 ).then_inc(x1_tail, 16)
            sp.wait_ge(out_done, 16 * HALVES * GROUPS + 16)

            def state_back(slot):
                sp.wait_ge(y_out[slot], 64 * GROUPS)
                for k in range(2):
                    sp.dma_start(tail_y(slot, k), y_piece[LG * HALVES + 2 * slot + k]).then_inc(y_tail[slot], 16)

            def results(slot):
                for k in range(2):
                    sp.wait_ge(add_tail[slot], k + 1)
                    sp.dma_start(out_piece[LG * HALVES + 2 * slot + k], z[slot][:, k * PIECE:(k + 1) * PIECE]
                                 ).then_inc(out_tail, 16)

            store_state(LG, 0)
            state_back(0)
            store_state(LG, 1)
            results(0)
            state_back(1)
            results(1)
            sp.wait_ge(out_tail, 16 * HALVES)
            for slot in range(SLOTS):
                sp.wait_ge(xa_in[slot], 64 * GROUPS)
            sp.wait_ge(xs_in, 16 * (first_place(HALVES * GROUPS) + 1))
            sp.wait_ge(x1_out, 16 * first_place(HALVES * GROUPS) + 16)

        @block.gpsimd
        def _(pool):
            def rsqrt(slot, kind, n):
                pool.wait_ge(post_done, NPOST * n + 2)
                nc.gpsimd.tensor_tensor(col(small, slot, kind, RSTD), col(small, slot, kind, VE),
                                        half[:, 0:1], ALU.pow).then_inc(pow_done, 1)

            def zero_rim(slot, lo, rim, own):
                v = hb[slot][:].rearrange("p l (i j) -> p l i j", j=PB)
                for k, (r0, rows) in enumerate(zip(offsets(PARTS_B), PARTS_B)):
                    part, first, last = slice(r0, r0 + rows), slice(0, 1), slice(NB - 1, NB)
                    places = [(0, 64, part, first), (64, 128, part, last)]
                    if k == 0:
                        places += [(0, 32, first, slice(0, NB)), (64, 96, first, slice(0, NB))]
                    if k == NP - 1:
                        places += [(32, 64, last, slice(0, NB)), (96, 128, last, slice(0, NB))]
                    pool.wait_ge(lo_done, lo + k + 1)
                    pool.sem_inc(pool_gate, 1)
                    for m, (p0, p1, ri, rj) in enumerate(places):
                        ins = nc.gpsimd.memset(v[p0:p1, :, ri, rj], 0.0)
                        if m < len(places) - 1:
                            ins.then_inc(pz, 1)
                            own = own + 1
                            pool.wait_ge(pz, own)
                        else:
                            ins.then_inc(rim_zero, 1)
                            pool.wait_ge(rim_zero, rim + k + 1)
                        pool.sem_inc(pool_gate, 1)

            def per_channel(v):
                return v.rearrange("p (c o) -> p c o", o=1).broadcast_to([H, CQ, H])

            def half_rsqrt(n, m):
                pool.wait_ge(s_m0, NHALF_STEPS * (n + 1))
                nc.gpsimd.tensor_tensor(m[:, 4, 0:CQ], m[:, 3, CQ:2 * CQ], half[0:H, :], ALU.pow).then_inc(pow0, 1)

            def centre_half():
                nc.gpsimd.tensor_tensor(xn[:], xs[:], per_channel(m0[:, 2, 0:CQ]), ALU.subtract).then_inc(s_xn, 1)

            def scale_half(n):
                pool.wait_ge(s_xn, 2 * first_place(n) + 1)
                pool.wait_ge(pow0, n + 1)
                nc.gpsimd.tensor_tensor(xn[:], xn[:], per_channel(m0[:, 4, 0:CQ]), ALU.mult).then_inc(s_xn, 1)

            def last_add(n):
                pool.wait_ge(fin_in, 32 * n + 32)
                o = fin[:, 2, :].rearrange("p (n j r) -> p n r j", j=NA, r=2)
                a = fin[:, 0, :].rearrange("p (n r j) -> p n r j", j=NA, r=2)
                b = fin[:, 1, :].rearrange("p (n r j) -> p n r j", j=NA, r=2)
                nc.gpsimd.tensor_tensor(o, a, b, ALU.add).then_inc(add_done, 1)

            def setup():
                for slot in range(SLOTS):
                    pool.memset(z[slot][:, NB * NB:], 0.0).then_inc(pool_set, 1)
                    pool.memset(ha[slot][:], 0.0).then_inc(pool_set, 1)
                pool.wait_ge(s_max, 1)
                for conv in range(2):
                    nc.gpsimd.partition_all_reduce(epsc[:, conv:conv + 1], small[:, 0, conv, 0:1], 128, RMAX
                                                   ).then_inc(pool_set, 1)

            pool.memset(half[:], -0.5).then_inc(pool_set, 1)
            pool.wait_ge(pool_set, 1)
            pool.sem_inc(add_done, HALVES + 1)
            for image in range(SLOTS):
                half_rsqrt(2 * image, m0)
                centre_half()
                half_rsqrt(2 * image + 1, m0b)
                pool.wait_ge(s_xn, 2 * image + 1)
                nc.gpsimd.tensor_tensor(xn[:], xn[:], per_channel(m0[:, 4, 0:CQ]), ALU.mult).then_inc(s_xn, 1)
                if image == 0:
                    setup()
            pool.wait_ge(pool_set, 1 + 2 * SLOTS + 2)
            for slot in range(SLOTS):
                rsqrt(slot, IZ, 2 * slot)
                rsqrt(slot, IY, 2 * slot + 1)

            PZ = 8

            def step(g, s, kind):
                lo, rim = parts_before(g, s), 2 * NP * (STEPS * g + s)
                own = 2 * PZ * (STEPS * g + s)
                first = posts_before(g, s, kind)
                for n, (what, slot) in enumerate(POSTS[kind]):
                    rsqrt(slot, what, first + n)
                    if what == Z1:
                        zero_rim(slot, lo + NP * slot, rim + NP * slot, own + PZ * slot)
                    if kind == MID and (what, slot) == (Z2, 0):
                        half_rsqrt(HALVES * (g + 1) + s, m0)
                        centre_half()
                    if kind == MID and (what, slot) == (Y, 0):
                        scale_half(HALVES * (g + 1) + s)
                if kind == MID:
                    with pool.If(g > 0):
                        last_add(g * HALVES + s)

            with pool.Fori(0, GROUPS - 1) as g:
                with pool.Fori(0, HALVES) as s:
                    step(g, s, MID)
                step(g, 4, FOUR)
                step(g, 5, FIVE)
            with pool.Fori(0, HALVES) as s:
                step(GROUPS - 1, s, LAST_MID)
                last_add((GROUPS - 1) * HALVES + s)
            step(GROUPS - 1, 4, LAST_MID)
            step(GROUPS - 1, 5, LAST)
            pool.wait_ge(x1_tail, 16 * HALVES)
            pool.wait_ge(y_tail[0], 32)
            for k in range(2):
                tail_sum(nc.gpsimd, 0, k)

        @block.scalar
        def _(act):
            def set_bias(conv, t, n):
                src = cbias[:, conv, t:t + 1] if isinstance(t, int) else cbias[:, conv, bass.ds(t, 1)]
                nc.scalar.activation(bias_now[:, conv:conv + 1], src, ACT.Identity).then_inc(bias_set, 1)
                act.wait_ge(bias_set, n + 1)

            def evacuate(slot, conv, k, i, n):
                rows = (TILES1, TILES2)[conv]
                width = (NB, NA)[conv]
                r0, r = offsets(rows)[k], rows[k]
                act.wait_ge(tile_done, n + i + 1)
                nc.scalar.activation(z[slot][:, r0 * width:(r0 + r) * width], cps[i % BANKS][:, 0:r * width],
                                     ACT.Identity, bias=bias_now[:, conv:conv + 1]).then_inc(evac_done, 1)

            def activate(slot, kind, k):
                if kind == Z1:
                    lo = offsets(PARTS_B)[k] * NB
                    n = PARTS_B[k] * NB
                else:
                    lo = offsets(PARTS_A)[k] * NA
                    n = PARTS_A[k] * NA
                src = {Z1: z, Y: y, IY: xa}[kind][slot]
                nc.scalar.activation(z[slot][:, lo:lo + n], src[:, lo:lo + n], ACT.Relu,
                                     bias=col(small, slot, kind, BI), scale=col(small, slot, kind, SC)
                                     ).then_inc(r_done, 1)

            def start_state(slot, n, post):
                act.wait_ge(post_done, post)
                nc.scalar.activation(xa[slot][:], xa[slot][:], ACT.Identity, bias=col(small, slot, IZ, BI),
                                     scale=col(small, slot, IZ, SC), accum_out=isum[:, slot, 0:1]
                                     ).then_inc(y0_done, 1)

            def start_squares(slot, n, adds=None):
                act.wait_ge(y0_done, n + 1)
                act.wait_ge(isq_done, n + 1)
                unread = z[1][:, 0:NA * NA]
                if adds is not None:
                    act.wait_ge(add_done, adds)
                    unread = fin[:, 0:2, :].rearrange("p a n -> p (a n)")
                nc.scalar.activation(unread, xa[slot][:], ACT.Square,
                                     accum_out=isum[:, slot, 1:2]).then_inc(isq_done, 1)

            def batch_copy(b, n):
                act.wait_ge(t_done, n + 1)
                nc.scalar.copy(ts[:, b % 2, :, :].rearrange("p c k -> p (c k)"), tps[0:H, 0:4 * H]
                               ).then_inc(ts_done, 1)

            act.sem_inc(isq_done, 1)
            act.sem_inc(ts_done, 1)
            with act.Fori(0, HALVES) as n:
                for b in range(NBATCH):
                    batch_copy(b, NBATCH * n + b)
            start_state(0, 0, NPOST)
            start_squares(0, 0)
            act.wait_ge(set_done, 1)
            act.wait_ge(post_done, NPOST * 2)
            for k in range(NP):
                activate(0, IY, k)
            set_bias(0, 0, 0)
            for k in range(8):
                evacuate(0, 0, k, k, 0)
                if k == 4:
                    start_state(1, 1, NPOST * 3)
                    start_squares(1, 1)
            act.wait_ge(post_done, NPOST * 4)
            for k in range(NP):
                activate(1, IY, k)

            def step(g, s, kind):
                n = tiles_before(g, s) - 8
                sq = 2 * NP * (5 * g + s)
                yup = 2 * NP * (STEPS * g + s)

                def posted(what, slot):
                    return NPOST * (posts_before(g, s, kind) + POSTS[kind].index((what, slot)) + 1)

                def final_state(slot, k):
                    act.wait_ge(yup_done, yup + NP * slot + 2 * k + 2)
                    act.wait_ge(post_done, posted(Z2, slot))
                    lo, m = k * NA * NA // 2, NA * NA // 2
                    nc.scalar.activation(y[slot][:, lo:lo + m], y[slot][:, lo:lo + m], ACT.Identity,
                                         bias=last_shift[:, slot:slot + 1]).then_inc(fin_done, 1)

                changes = 1 + 2 * (STEPS * g + s)
                i = 8
                for phase, (slot, other, conv) in enumerate(((1, 0, 0), (0, 1, 1))):
                    if conv == 1:
                        set_bias(1, s, changes)
                    for k in range(len((TILES1, TILES2)[conv])):
                        evacuate(slot, conv, k, i, n)
                        i += 1
                        if k == 1:
                            act.wait_ge(post_done, posted(Z1, other))
                        if 1 <= k <= NP:
                            activate(other, Z1, k - 1)
                        if kind == FIVE and phase == 0 and k == 0:
                            start_state(0, SLOTS * (g + 1), NPOST * (posts_before(g, 4, FOUR) + POSTS[FOUR].index((IZ, 0)) + 1))
                        if kind == FIVE and phase == 1 and k == 0:
                            start_state(1, SLOTS * (g + 1) + 1, posted(IZ, 1))
                        if kind == FIVE and k == (6, 5)[phase]:
                            start_squares(phase, SLOTS * (g + 1) + phase, HALVES * (g + 1) + 1)
                for phase, (slot, other, conv) in enumerate(((1, 0, 1), (0, 1, 0))):
                    if kind == LAST and phase == 1:
                        for k in range(2):
                            final_state(1, k)
                        break
                    if conv == 0:
                        set_bias(0, s + 1 if kind != FIVE else 0, changes + 1)
                    tiles = len((TILES1, TILES2)[conv])
                    for k in range(tiles):
                        evacuate(slot, conv, k, i, n)
                        i += 1
                        if kind == MID and phase == 1 and 1 <= k <= NBATCH:
                            batch_copy(k - 1, NBATCH * (HALVES * (g + 1) + s) + k - 1)
                        if kind not in (FIVE, LAST) and k in (1, 2):
                            for part in (2 * k - 2, 2 * k - 1):
                                act.wait_ge(yup_done, yup + NP * other + part + 1)
                                lo, m = offsets(PARTS_A)[part] * NA, PARTS_A[part] * NA
                                nc.scalar.activation(z[other][:, lo:lo + m], y[other][:, lo:lo + m], ACT.Square,
                                                     accum_out=ysum[:, other, part, 1:2]).then_inc(sq_done, 1)
                        if kind == LAST:
                            if k in (2, 3):
                                final_state(0, k - 2)
                            continue
                        if k == 4:
                            if kind == FIVE:
                                act.wait_ge(yup_done, yup + NP * other + NP)
                                act.wait_ge(post_done, posted(*((IY, 0) if other == 0 else (IY, 1))))
                            else:
                                act.wait_ge(post_done, posted(Y, other))
                        for part in {4: (0, 1), 5: (2,), 6: (3,)}.get(k, ()):
                            activate(other, IY if kind == FIVE else Y, part)
                        if kind == FIVE and k >= tiles - 2:
                            final_state(other, k - tiles + 2)

            with act.Fori(0, GROUPS - 1) as g:
                with act.Fori(0, HALVES) as s:
                    step(g, s, MID)
                step(g, 4, FOUR)
                step(g, 5, FIVE)
            with act.Fori(0, STEPS - 1) as s:
                step(GROUPS - 1, s, LAST_MID)
            step(GROUPS - 1, 5, LAST)

        @block.vector
        def _(dve):
            chain = [0]

            def link(ins):
                chain[0] += 1
                ins.then_inc(s_set, 1)
                dve.wait_ge(s_set, chain[0])

            def go(ins):
                chain[0] += 1
                ins.then_inc(s_set, 1)

            def settled():
                dve.wait_ge(s_set, chain[0])

            wsrc = z[0][:, 0:576].rearrange("p (v n) -> p v n", v=2)
            w0v = z[1][:, 0:256].rearrange("p (v n) -> p v n", v=2)
            wi = z[0][:, 1000:1576].rearrange("p (v n) -> p v n", v=2)
            sm = small[:, 1, :, :].rearrange("p a b -> p (a b)")
            scale = sm[:, 42:44]
            ab, neg, bound, fl, inv = sm[:, 0:8], sm[:, 8:16], sm[:, 16:18], sm[:, 18:20], sm[:, 20:22]
            mx, nmx = sm[:, 22:30], sm[:, 30:38]
            s_fl, s_inv = sm[:, 38:40], sm[:, 40:42]

            def setup_bounds():
                dve.wait_ge(setup_in, 16 * 7)
                go(nc.vector.tensor_scalar(gb[:, 4:5], prm[:, G3:G3 + 1], DT, None, ALU.mult))
                go(nc.vector.tensor_scalar(gb[:, 5:6], prm[:, B3:B3 + 1], DT, float(STEPS), ALU.mult, ALU.mult))
                link(nc.vector.tensor_scalar(neg, prm[:], -1.0, None, ALU.mult))
                link(nc.vector.tensor_tensor(ab, prm[:], neg, ALU.max))
                for conv, (gm, bt) in enumerate(((G1, B1), (G2, B2))):
                    go(nc.vector.tensor_scalar(bound[:, conv:conv + 1], ab[:, gm:gm + 1], float(H), ab[:, bt:bt + 1],
                                               ALU.mult, ALU.add))
                settled()
                power_of_two(bound, fl, inv)
                for conv, (gm, bt) in enumerate(((G1, B1), (G2, B2))):
                    for j in (0, 1):
                        go(nc.vector.tensor_scalar(gb[:, 2 * conv + j:2 * conv + j + 1],
                                                   prm[:, (gm, bt)[j]:(gm, bt)[j] + 1], inv[:, conv:conv + 1],
                                                   2.0 ** 13, ALU.mult, ALU.mult))
                    go(nc.vector.tensor_scalar(wi[:, conv, :], wsrc[:, conv, :], fl[:, conv:conv + 1], 2.0 ** -13,
                                               ALU.mult, ALU.mult))
                settled()
                for k, (src, op) in enumerate(((wi, ALU.max), (wi, ALU.min), (w0v, ALU.max), (w0v, ALU.min))):
                    go(nc.vector.tensor_reduce(mx[:, 2 * k:2 * k + 2], src, AX_X, op))
                settled()
                link(nc.vector.tensor_scalar(nmx, mx, -1.0, None, ALU.mult))
                link(nc.vector.tensor_tensor(mx, mx, nmx, ALU.max))
                nc.vector.tensor_reduce(small[:, 0, 0:2, 0], mx.rearrange("p (k v) -> p v k", v=2), AX_X, ALU.max
                                        ).then_inc(s_max, 1)

            def setup_weights():
                go(nc.vector.memset(rim_w[:], 0.0))
                go(nc.vector.memset(w1[:], 0.0))
                go(nc.vector.memset(w2[:], 0.0))
                dve.wait_ge(pool_set, 1 + 2 * SLOTS + 2)
                power_of_two(epsc[:, 0:2], s_fl, s_inv)
                link(nc.vector.tensor_scalar(scale, s_inv, 2.0 ** 13, None, ALU.mult))
                dve.wait_ge(s_rimps, 1)
                gs = z[0][:, 600:856].rearrange("p (v n) -> p v n", v=2)
                box, cb = sm[:, 8:10], sm[:, 10:12]
                for conv in range(2):
                    at = scale[:, conv:conv + 1]
                    go(nc.vector.tensor_scalar(gb[:, 6 + conv:7 + conv], at, at, EPS, ALU.mult, ALU.mult))
                    go(nc.vector.tensor_scalar(wi[:, conv, :], wi[:, conv, :], at, None, ALU.mult))
                    go(nc.vector.tensor_scalar(gs[:, conv, :], cps[conv][:, 0:128], at, None, ALU.mult))
                    go(nc.vector.tensor_scalar(box[:, conv:conv + 1], cps[2 + conv][:, 0:1], at, None, ALU.mult))
                    go(nc.vector.tensor_scalar(cb[:, conv:conv + 1], prm[:, CB1 + conv:CB1 + conv + 1], at, None,
                                               ALU.mult))
                settled()
                hi = hb[0][:, 0, 0:1152].rearrange("p (v l n) -> p v l n", v=2, l=2)
                gk = z[0][:, 1600:1600 + 2 * STEPS * 128].rearrange("p (v k n) -> p v k n", v=2, k=STEPS)
                gh = hb[0][:, 1, 0:2 * STEPS * 128].rearrange("p (v k n) -> p v k n", v=2, k=STEPS)
                go(nc.vector.tensor_copy(hi[:, :, 0, :], wi))
                for k in range(STEPS):
                    t = float(np.float32(DT) * np.float32(k))
                    for conv in range(2):
                        go(nc.vector.tensor_scalar(cbias[:, conv, k:k + 1], box[:, conv:conv + 1], t,
                                                   cb[:, conv:conv + 1], ALU.mult, ALU.add))
                    go(nc.vector.tensor_scalar(gk[:, :, k, :], gs, t, None, ALU.mult))
                settled()
                go(nc.vector.tensor_tensor(hi[:, :, 1, :], wi, hi[:, :, 0, :], ALU.subtract))
                go(nc.vector.tensor_copy(gh, gk))
                settled()
                go(nc.vector.tensor_copy(rim_w[0:32], gh[0:32]))
                go(nc.vector.tensor_tensor(rim_w[32:64], gk[32:64], gh[32:64], ALU.subtract))
                settled()

            def place_weights(conv, q):
                w = (w1, w2)[conv]
                hl = hb[0][:, 0, 576 * conv:576 * (conv + 1)].rearrange("p (l k o) -> p l k o", l=2, k=9)
                ix, iy = q // 2, q % 2
                for a in range(2):
                    for b in range(2):
                        for qo in range(4):
                            ox, oy = qo // 2, qo % 2
                            ky, kx = 2 * a + iy - oy, 2 * b + ix - ox
                            if 0 <= ky < 3 and 0 <= kx < 3:
                                last = nc.vector.tensor_copy(
                                    w[q * C:(q + 1) * C, 2 * a + b, :, qo * C:(qo + 1) * C],
                                    hl[q * C:(q + 1) * C, :, 3 * ky + kx, :])
                go(last)

            def finish_setup():
                for slot in range(SLOTS):
                    go(nc.vector.tensor_copy(shift[:, slot:slot + 1], gb[:, 5:6]))
                settled()
                nc.vector.tensor_copy(epsc[:], gb[:, 6:8]).then_inc(set_done, 1)

            def power_of_two(v, fl, inv):
                link(nc.vector.tensor_scalar(v, v, 1e-18, 1e18, ALU.max, ALU.min))
                link(nc.vector.tensor_scalar(fl.bitcast(I32), v.bitcast(I32), 0x7F800000, None, ALU.bitwise_and))
                link(nc.vector.tensor_scalar(inv.bitcast(I32), fl.bitcast(I32), -1.0, float(254 << 23),
                                             ALU.mult, ALU.add))

            def tile_stats(slot, conv, k, n):
                dve.wait_ge(evac_done, n + 1)
                if conv == 1:
                    r0, r = offsets(TILES2)[k], TILES2[k]
                    ins = nc.vector.bn_stats(bn[slot][:, k, :], z[slot][:, r0 * NA:(r0 + r) * NA])
                    if k == 6:
                        ins.then_inc(bn_done, 1)
                    return
                r0, r = offsets(TILES1)[k], TILES1[k]
                a, b = max(r0, 1), min(r0 + r, NB - 1)
                v = z[slot][:, 0:NB * NB].rearrange("p (i j) -> p i j", j=NB)
                nc.vector.bn_stats(bn[slot][:, k, :], v[:, a:b, 1:NB - 1])
                if k == 0:
                    nc.vector.bn_stats(bn[slot][32:64, 8, :], v[32:64, 0, 1:NB])
                    nc.vector.bn_stats(bn[slot][96:128, 8, :], v[96:128, 0, 0:NB - 1])
                if k == 7:
                    nc.vector.bn_stats(bn[slot][0:32, 8, :], v[0:32, NB - 1, 1:NB])
                    nc.vector.bn_stats(bn[slot][64:96, 8, :], v[64:96, NB - 1, 0:NB - 1])
                    nc.vector.bn_stats(bn[slot][64:128, 9, :], v[64:128, 1:NB - 1, 0])
                    nc.vector.bn_stats(bn[slot][0:64, 9, :], v[0:64, 1:NB - 1, NB - 1]).then_inc(bn_done, 1)

            def pre(slot, kind, groups, n):
                src = (bni if kind == IZ else bn)[slot]
                dve.sem_inc(dve_gate, 1)
                nc.vector.bn_aggr(col(small, slot, kind, MEAN, 2), src[:, 0:groups, :].rearrange("p a b -> p (a b)")
                                  ).then_inc(pre_done, 1)
                dve.wait_ge(pre_done, 2 * n + 1)
                nc.vector.scalar_tensor_tensor(out=col(small, slot, kind, E2), in0=col(small, slot, kind, MEAN),
                                               scalar=col(small, slot, kind, MEAN), in1=col(small, slot, kind, E2),
                                               op0=ALU.mult, op1=ALU.add).then_inc(pre_done, 1)

            def post(slot, kind, ev, n, last=False, meanwhile=None):
                done = NPOST * n
                eps = {Z1: gb[:, 6:7], Z2: gb[:, 7:8]}.get(kind, EPS)
                gamma = {Z1: gb[:, 2:3], Z2: gb[:, 4:5], Y: gb[:, 0:1], IY: gb[:, 0:1], IZ: 1.0}[kind]
                beta = {Z1: gb[:, 3:4], Z2: shift[:, slot:slot + 1], Y: gb[:, 1:2], IY: gb[:, 1:2],
                        IZ: zero[:, 0:1]}[kind]
                bias = col(small, slot, kind, BI)
                if kind == Z2:
                    bias = (last_shift if last else shift)[:, slot:slot + 1]
                dve.wait_ge(stat_done, ev + 1)
                if kind == Y:
                    nc.vector.tensor_reduce(col(small, slot, kind, MS, 2),
                                            sps[:, 0:2 * NP].rearrange("p (k n) -> p n k", n=2), AX_X, ALU.add
                                            ).then_inc(stat_read, 1)
                else:
                    nc.vector.tensor_copy(col(small, slot, kind, MS, 2), sps[:, 0:2]).then_inc(stat_read, 1)
                dve.wait_ge(stat_read, ev + 2)
                nc.vector.scalar_tensor_tensor(out=col(small, slot, kind, VAR), in0=col(small, slot, kind, MS),
                                               scalar=col(small, slot, kind, MS), in1=col(small, slot, kind, ES),
                                               op0=ALU.mult, op1=ALU.subtract, reverse1=True).then_inc(post_done, 1)
                dve.wait_ge(post_done, done + 1)
                nc.vector.tensor_scalar(col(small, slot, kind, VE), col(small, slot, kind, VAR), 0.0, eps,
                                        ALU.max, ALU.add).then_inc(post_done, 1)
                if meanwhile:
                    meanwhile()
                dve.wait_ge(pow_done, n + 1)
                nc.vector.tensor_scalar(col(small, slot, kind, SC), col(small, slot, kind, RSTD), gamma, None,
                                        ALU.mult).then_inc(post_done, 1)
                dve.wait_ge(post_done, done + 3)
                nc.vector.scalar_tensor_tensor(out=bias, in0=col(small, slot, kind, MS),
                                               scalar=col(small, slot, kind, SC), in1=beta,
                                               op0=ALU.mult, op1=ALU.subtract, reverse1=True).then_inc(post_done, 1)
                if kind == Z2:
                    dve.wait_ge(post_done, done + NPOST)

            def split(slot, grid_b, k, n, halves=(0, 1)):
                rows = PARTS_B if grid_b else PARTS_A
                width = NB if grid_b else NA
                r0, r = offsets(rows)[k], rows[k]
                if grid_b:
                    r += r % 2
                src = z[slot][:, r0 * width:(r0 + r) * width].rearrange("p (i j) -> p i j", j=width)
                if grid_b:
                    v = hb[slot][:].rearrange("p l (i j) -> p l i j", j=PB)[:, :, r0:r0 + r, 0:NB]
                else:
                    v = ha[slot][:].rearrange("p l (i j) -> p l i j", j=PADA)[:, :, r0 + 1:r0 + r + 1, 1:NA + 1]
                if 0 in halves:
                    dve.wait_ge(r_done, n + k + 1)
                    nc.vector.tensor_copy(v[:, 0], src).then_inc(hi_done, 1)
                if 1 in halves:
                    dve.wait_ge(hi_done, n + k + 1)
                    nc.vector.tensor_tensor(v[:, 1], src, v[:, 0], ALU.subtract).then_inc(lo_done, 1)

            def euler(slot, k, last):
                lo, m = offsets(PARTS_A)[k] * NA, PARTS_A[k] * NA
                acc = {} if last else {"accum_out": ysum[:, slot, k, 0:1]}
                nc.vector.scalar_tensor_tensor(out=y[slot][:, lo:lo + m], in0=z[slot][:, lo:lo + m],
                                               scalar=col(small, slot, Z2, SC), in1=y[slot][:, lo:lo + m],
                                               op0=ALU.mult, op1=ALU.add, **acc).then_inc(yup_done, 1)

            def start_stats(slot, n, tiles):
                if tiles[0] == 0:
                    dve.wait_ge(xa_in[slot], 64 * n + 64)
                for k in tiles:
                    ins = nc.vector.bn_stats(bni[slot][:, k, :], xa[slot][:, k * 448:(k + 1) * 448])
                if tiles[-1] == 6:
                    ins.then_inc(ibn_done, 1)

            def half_stats(channels, buffers=FIRST):
                src, _, _, bn0, _ = buffers
                for c in channels:
                    ins = nc.vector.bn_stats(bn0[:, c, :], src[:, c, :])
                if channels[-1] == CQ - 1:
                    ins.then_inc(s_m0, 1)

            def half_pre(n, buffers=FIRST):
                bn0, m0 = buffers[3:]
                b = NHALF_STEPS * n
                dve.wait_ge(s_m0, b + 1)
                me, ve, mo, vo = (bn0[:, :, k] for k in (1, 2, 4, 5))
                nc.vector.tensor_tensor(m0[:, 0, 0:CQ], me, mo, ALU.add).then_inc(s_m0, 1)
                nc.vector.tensor_tensor(m0[:, 1, 0:CQ], ve, vo, ALU.add).then_inc(s_m0, 1)
                nc.vector.tensor_tensor(m0[:, 1, CQ:2 * CQ], me, me, ALU.mult).then_inc(s_m0, 1)
                nc.vector.tensor_tensor(m0[:, 5, 0:CQ], mo, mo, ALU.mult).then_inc(s_m0, 1)
                dve.wait_ge(s_m0, b + 5)
                nc.vector.tensor_tensor(m0[:, 5, CQ:2 * CQ], m0[:, 5, 0:CQ], m0[:, 1, CQ:2 * CQ], ALU.add
                                        ).then_inc(s_m0, 1)
                dve.wait_ge(s_m0, b + 6)
                nc.vector.scalar_tensor_tensor(out=m0[:, 0, CQ:2 * CQ], in0=m0[:, 1, 0:CQ], scalar=2.0 / H,
                                               in1=m0[:, 5, CQ:2 * CQ], op0=ALU.mult, op1=ALU.add).then_inc(s_m0, 1)

            def half_post(n, ev, buffers=FIRST):
                m0 = buffers[4]
                b = NHALF_STEPS * n
                dve.wait_ge(stat_done, ev + 1)
                nc.vector.tensor_copy(m0[:, 2, :], sps[0:H, 0:2 * CQ]).then_inc(stat_read, 1)
                dve.wait_ge(stat_read, ev + 2)
                nc.vector.tensor_tensor(m0[:, 3, 0:CQ], m0[:, 2, 0:CQ], m0[:, 2, 0:CQ], ALU.mult).then_inc(s_m0, 1)
                dve.wait_ge(s_m0, b + 8)
                nc.vector.tensor_tensor(m0[:, 4, CQ:2 * CQ], m0[:, 2, CQ:2 * CQ], m0[:, 3, 0:CQ], ALU.subtract
                                        ).then_inc(s_m0, 1)
                dve.wait_ge(s_m0, b + 9)
                nc.vector.tensor_scalar(m0[:, 3, CQ:2 * CQ], m0[:, 4, CQ:2 * CQ], 0.0, EPS, ALU.max, ALU.add
                                        ).then_inc(s_m0, 1)

            def half_add(b, n, buffers=FIRST):
                dve.wait_ge(xp_done, n + 1)
                xs, _, x1s = buffers[:3]
                xv = xs[:, 4 * b:4 * b + 4, :].rearrange("p c (j r) -> p c r j", r=2)
                nc.vector.tensor_tensor(x1s[:, 4 * b:4 * b + 4], xps[0:H, 0:4 * H].rearrange(
                    "p (c r j) -> p c r j", c=4, r=2), xv, ALU.add).then_inc(x1_done, 1)

            dve.sem_inc(x1_done, 1)
            dve.sem_inc(stat_read, 1)
            go(nc.vector.memset(zero[:], 0.0))
            go(nc.vector.memset(ones[:], 1.0))
            for image in range(SLOTS):
                for k, (buffers, arrived) in enumerate(((FIRST, xs_in), (SECOND, xsb_in))):
                    dve.wait_ge(arrived, 16 * (image + 1))
                    half_stats(range(CQ), buffers)
                    half_pre(2 * image + k, buffers)
                    half_post(2 * image + k, 2 * image + k, buffers)
                mean, rstd = (m0b[:, k, 0:CQ].rearrange("p (c o) -> p c o", o=1).broadcast_to([H, CQ, H])
                              for k in (2, 4))
                nc.vector.tensor_tensor(xnb, xsb, mean, ALU.subtract).then_inc(s_xnb, 1)
                if image == 0:
                    setup_bounds()
                else:
                    setup_weights()
                dve.wait_ge(s_xnb, 2 * image + 1)
                dve.wait_ge(pow0, 2 * image + 2)
                nc.vector.tensor_tensor(xnb, xnb, rstd, ALU.mult).then_inc(s_xnb, 1)
                for k, (buffers, left) in enumerate(((FIRST, x1_out), (SECOND, x1b_out))):
                    if image > 0:
                        dve.wait_ge(left, 16 * image + (16, 0)[k])
                    for b in range(NBATCH):
                        if image == 1:
                            place_weights(k, b)
                            if NBATCH * k + b < 7:
                                start_stats(0, 0, (NBATCH * k + b,))
                        half_add(b, NBATCH * (2 * image + k) + b, buffers)
            dve.wait_ge(ibn_done, 1)
            pre(0, IZ, 7, 0)
            post(0, IZ, HALVES, 0)
            finish_setup()
            post(0, IY, HALVES + 1, 1)
            for k in range(NP):
                split(0, False, k, 0)
            for k in range(8):
                tile_stats(0, 0, k, k)
                if k == 3:
                    start_stats(1, 0, range(7))
                    dve.wait_ge(ibn_done, 2)
                    pre(1, IZ, 7, 1)
                    post(1, IZ, HALVES + 2, 2)
            post(1, IY, HALVES + 3, 3)
            for k in range(NP - 1):
                split(1, False, k, NP)

            def step(g, s, kind):
                n = tiles_before(g, s) - 8
                parts = parts_before(g, s)
                bns = 1 + 4 * (STEPS * g + s)
                hn = HALVES * (g + 1) + s

                def pre_of(what, slot, groups):
                    pre(slot, what, groups, pres_before(g, s, kind) + PRES[kind].index((what, slot)))

                def post_of(what, slot, last=False, meanwhile=None):
                    post(slot, what, stats_before(g, s, kind) + STATS[kind].index((what, slot)),
                         posts_before(g, s, kind) + POSTS[kind].index((what, slot)), last, meanwhile)

                i = 8
                for phase, (slot, other, conv) in enumerate(((1, 0, 0), (0, 1, 1))):
                    dve.wait_ge(bn_done, bns + phase)
                    pre_of(Z1, other, 10)
                    for k in range(len((TILES1, TILES2)[conv])):
                        tile_stats(slot, conv, k, n + i)
                        i += 1
                        if k == 0:
                            if phase == 0:
                                post_of(Z1, other, meanwhile=lambda: split(1, False, 3, parts - NP, (0,)))
                                split(1, False, 3, parts - NP, (1,))
                            elif kind == MID:
                                post_of(Z1, other, meanwhile=lambda: half_stats(range(12, CQ)))
                            else:
                                post_of(Z1, other)
                        if 1 <= k <= 4:
                            split(other, True, k - 1, parts + NP * phase)
                        if kind == MID and phase == 0 and 2 <= k <= 7:
                            if k == 2:
                                dve.wait_ge(xs_in, 16 * first_place(hn) + 16)
                            half_stats(range(2 * (k - 2), 2 * (k - 1)))
                        if kind == MID and phase == 1 and k == 2:
                            half_pre(hn)
                        if kind == MID and phase == 1 and k == 6:
                            half_post(hn, stats_before(g, s, kind) + STATS[MID].index((X0, 0)))
                        if kind == FOUR and phase == 1 and k >= 5:
                            start_stats(0, g + 1, range(2 * (k - 5), 2 * (k - 4)))
                        if kind == FIVE and phase == 0 and k == 1:
                            dve.wait_ge(ibn_done, SLOTS * (g + 1) + 2)
                            pre_of(IZ, 1, 7)
                        if kind == FIVE and phase == 0 and k == 7:
                            post_of(IZ, 1)
                        if kind == FIVE and phase == 1 and k == 5:
                            post_of(IY, 0)
                held, first = (2, (0, 1)) if kind == MID else (3, (0,))
                for phase, (slot, other, conv) in enumerate(((1, 0, 1), (0, 1, 0))):
                    dve.wait_ge(bn_done, bns + 2 + phase)
                    pre_of(Z2, other, 7)
                    if kind == LAST and phase == 1:
                        post_of(Z2, 1, True)
                        for part in range(NP):
                            euler(1, part, True)
                        break
                    state = parts + 2 * NP + NP * phase
                    for k in range(len((TILES1, TILES2)[conv])):
                        if kind == MID and phase == 1 and 3 <= k < 3 + NBATCH:
                            if k == 3:
                                dve.wait_ge(x1_out, 16 * first_place(hn) + 16)
                            half_add(k - 3, NBATCH * hn + k - 3)
                        tile_stats(slot, conv, k, n + i)
                        i += 1
                        if k == 0:
                            post_of(Z2, other, kind in (FIVE, LAST),
                                    meanwhile=(lambda: split(0, False, held, state - NP, first)) if phase == 1 else
                                    (lambda: start_stats(0, g + 1, (4, 5))) if kind == FOUR else None)
                            if kind == FIVE:
                                nc.vector.tensor_copy(shift[:, other:other + 1], gb[:, 5:6]).then_inc(shift_set, 1)
                                dve.wait_ge(shift_set, SLOTS * g + phase + 1)
                            dve.wait_ge(y_new[other], 16 * (g + 1))
                        if phase == 1 and k == 2 and held == 2:
                            split(0, False, 3, state - NP)
                        if k == 0:
                            for part in range(NP):
                                euler(other, part, kind in (FIVE, LAST))
                                if phase == 1 and part == 1 and kind != MID:
                                    split(0, False, held, state - NP, (1,))
                        if kind == FOUR and phase == 0 and k == 4:
                            dve.wait_ge(ibn_done, SLOTS * (g + 1) + 1)
                            pre_of(IZ, 0, 7)
                        if kind in (MID, LAST_MID) and k == 3:
                            post_of(Y, other)
                        if kind == FOUR and k == 3:
                            part = ((6,), (4, 5))[phase]
                            post_of(Y, other, meanwhile=lambda: start_stats(phase, g + 1, part))
                        if kind == FIVE and phase == 0 and k == 4:
                            post_of(IY, 1)
                        if kind == FOUR and phase == 1 and k == 6:
                            post_of(IZ, 0, meanwhile=lambda: split(1, False, 2, state))
                        elif kind != LAST and 4 <= k <= (5 + phase if kind == MID else 6):
                            split(other, False, k - 4, state)
                        if kind == FOUR and (phase, k) in START_PLAN:
                            start_stats(1, g + 1, START_PLAN[phase, k])

            with dve.Fori(0, GROUPS - 1) as g:
                with dve.Fori(0, HALVES) as s:
                    step(g, s, MID)
                step(g, 4, FOUR)
                step(g, 5, FIVE)
            with dve.Fori(0, STEPS - 1) as s:
                step(GROUPS - 1, s, LAST_MID)
            step(GROUPS - 1, 5, LAST)
            dve.wait_ge(x1_tail, 16 * HALVES)
            dve.wait_ge(y_tail[1], 32)
            for k in range(2):
                tail_sum(nc.vector, 1, k)

        @block.tensor
        def _(pe):
            def rim_tables():
                pe.wait_ge(setup_in, 16 * 7)
                coef = z[1][:, 256:1280].rearrange("p (v q r) -> p v q r", v=2, q=4)
                w0v = z[1][:, 0:256].rearrange("p (v n) -> p v n", v=2)
                pe.wait_ge(s_set, 2)
                for conv in range(2):
                    for q in range(4):
                        pe.matmul(cps[conv][:, q * C:(q + 1) * C], coef[:, conv, q, :],
                                  w0v[:, conv, q * C:(q + 1) * C], start=True, stop=True)
                    last = pe.matmul(cps[2 + conv][:, 0:1], w0v[:, conv, :], ones[:, 0:1], start=True, stop=True)
                last.then_inc(s_rimps, 1)

            def conv_tile(slot, conv, k, i, t, between):
                rows = (TILES1, TILES2)[conv]
                r0, r = offsets(rows)[k], rows[k]
                width = (NB, NA)[conv]
                pitch = (PADA, PB)[conv]
                w = (w1, w2)[conv]
                h = (ha, hb)[conv][slot][:].rearrange("p l (i j) -> p l i j", j=pitch)
                ps = cps[i % BANKS][:, 0:r * width].rearrange("p (i j) -> p i j", j=width)
                products = [(tap, wl, hl) for wl, hl in ((0, 0), (0, 1), (1, 0)) for tap in range(4)]

                def product(n):
                    tap, wl, hl = products[n]
                    a, b = tap // 2, tap % 2
                    return pe.matmul(ps, w[:, tap, wl, :], h[:, hl, r0 + a:r0 + a + r, b:b + width],
                                     start=(n == 0), stop=(n == len(products) - 1))

                for m in range(len(products) - 1):
                    if (k, m) in between:
                        between[k, m]()
                    product(m)
                rw = rim_w[:, conv, t, :] if isinstance(t, int) else \
                    rim_w[:, conv, bass.ds(t, 1), :].rearrange("p a n -> p (a n)")
                at = (RIM1, RIM2)[conv]
                if k == 0:
                    pe.matmul(ps[:, 0, :], rw, rim_i[:, at:at + width], start=False, stop=False)
                if k == len(rows) - 1:
                    pe.matmul(ps[:, r - 1, :], rw, rim_i[:, at + width:at + 2 * width], start=False, stop=False)
                pe.matmul(ps[:, :, 0:width:width - 1], rw,
                          rim_i[:, RIMC:RIMC + 2 * r].rearrange("p (i j) -> p i j", j=2),
                          start=False, stop=False)
                product(len(products) - 1).then_inc(tile_done, 1)

            def needs(conv, k):
                rows = (TILES1, TILES2)[conv]
                parts = (PARTS_A, PARTS_B)[conv]
                last = offsets(rows)[k] + rows[k] + (0 if conv == 0 else 1)
                last = min(last, sum(parts))
                return next(p + 1 for p in range(NP) if offsets(parts)[p] + parts[p] >= last)

            def tile(slot, conv, k, i, n, t, ready, base, between=()):
                if k == 0 or needs(conv, k) > needs(conv, k - 1):
                    pe.wait_ge(ready, base + needs(conv, k))
                if not (isinstance(n, int) and n + i < BANKS):
                    pe.wait_ge(evac_done, n + i - BANKS + 1)
                conv_tile(slot, conv, k, i, t, between)

            def statistics(slot, kind, ev, wait, value):
                pe.wait_ge(stat_read, ev + 1)
                pe.wait_ge(wait, value)
                if kind in (Z1, Z2, IZ):
                    last = pe.matmul(sps[:, 0:2], mats[:, 0, :], col(small, slot, kind, MEAN, 2),
                                     start=True, stop=True)
                elif kind == IY:
                    last = pe.matmul(sps[:, 0:2], mats[:, 1, :], isum[:, slot, :], start=True, stop=True)
                else:
                    last = pe.matmul(sps[:, 0:2 * NP], mats[:, 1, :],
                                     ysum[:, slot].rearrange("p k n -> p (k n)"), start=True, stop=True)
                last.then_inc(stat_done, 1)

            def half_mean(n, ev, m0=m0):
                pe.wait_ge(stat_read, ev + 1)
                pe.wait_ge(s_m0, NHALF_STEPS * n + 7)
                pe.matmul(sps[0:H, 0:2 * CQ], mats[0:H, 2, 0:H], m0[:, 0, :], start=True, stop=True
                          ).then_inc(stat_done, 1)

            def dct_rows(b, n, xn=xn):
                pe.wait_ge(ts_done, n + 1)
                for c in range(4):
                    last = pe.matmul(tps[0:H, c * H:(c + 1) * H], xn[:, 4 * b + c, :], dct[:, 0, :],
                                     start=True, stop=True)
                last.then_inc(t_done, 1)

            def dct_columns(b, n):
                pe.wait_ge(ts_done, n + 2)
                pe.wait_ge(x1_done, n + 1)
                for c in range(4):
                    last = pe.matmul(xps[0:H, c * H:(c + 1) * H], ts[:, b % 2, c, :], dct[:, 1, :],
                                     start=True, stop=True)
                last.then_inc(xp_done, 1)

            def rows_of(b, hn):
                if b == 0:
                    pe.wait_ge(s_xn, 2 * first_place(hn) + 2)
                dct_rows(b, NBATCH * hn + b)

            rim_tables()
            for image in range(SLOTS):
                half_mean(2 * image, 2 * image)
                half_mean(2 * image + 1, 2 * image + 1, m0b)
                for k, (ready, src) in enumerate(((s_xn, xn), (s_xnb, xnb))):
                    n = NBATCH * (2 * image + k)
                    pe.wait_ge(ready, 2 * image + 2)
                    dct_rows(0, n, src)
                    for b in range(NBATCH):
                        if b < NBATCH - 1:
                            dct_rows(b + 1, n + b + 1, src)
                        dct_columns(b, n + b)
            statistics(0, IZ, HALVES, pre_done, 2)
            statistics(0, IY, HALVES + 1, isq_done, 2)
            pe.wait_ge(set_done, 1)
            for k in range(8):
                tile(0, 0, k, k, 0, 0, lo_done, 0,
                     {(6, 0): lambda: statistics(1, IZ, HALVES + 2, pre_done, 4)})
            statistics(1, IY, HALVES + 3, isq_done, 3)

            def step(g, s, kind):
                n = tiles_before(g, s) - 8
                parts = parts_before(g, s)
                rim = 2 * NP * (STEPS * g + s)
                sq = 2 * NP * (5 * g + s)
                hn = HALVES * (g + 1) + s

                def statistics_of(what, slot):
                    if what in (Z1, Z2, IZ):
                        wait, value = pre_done, 2 * (pres_before(g, s, kind) + PRES[kind].index((what, slot)) + 1)
                    elif what == IY:
                        wait, value = isq_done, SLOTS * (g + 1) + slot + 2
                    else:
                        wait, value = sq_done, sq + NP * (slot + 1)
                    statistics(slot, what, stats_before(g, s, kind) + STATS[kind].index((what, slot)), wait, value)

                def among(*places):
                    return {(k, m): (lambda e=event: statistics_of(*e)) for k, m, event in places}

                i = 8
                between = among((2, {MID: 1, FOUR: 1, FIVE: 10}.get(kind, 6), (Z1, 0)))
                if kind == FIVE:
                    between.update(among((7, 0, (IZ, 1))))
                for k in range(8):
                    tile(1, 0, k, i, n, s, lo_done, parts - NP, between)
                    i += 1
                between = among((2, 0, (Z1, 1)) if kind == FIVE else (1, 9, (Z1, 1)))
                if kind == MID:
                    between[5, 6] = lambda: half_mean(hn, stats_before(g, s, kind) + STATS[MID].index((X0, 0)))
                if kind == FIVE:
                    between.update(among((5, 0, (IY, 0))))
                for k in range(7):
                    tile(0, 1, k, i, n, s, rim_zero, rim, between)
                    i += 1
                between = among((1, 9 if kind == FIVE else 3, (Z2, 0)))
                if kind not in (FIVE, LAST):
                    between.update(among((4, 9, (Y, 0))))
                elif kind == FIVE:
                    between.update(among((4, 0, (IY, 1))))
                for k in range(7):
                    tile(1, 1, k, i, n, s, rim_zero, rim + NP, between)
                    i += 1
                if kind == LAST:
                    statistics_of(Z2, 1)
                    return
                between = among((1, 3, (Z2, 1)) if kind == MID else (2, 0, (Z2, 1)))
                if kind != FIVE:
                    between.update(among((4, 2, (Y, 1)) if kind == MID else (5, 8, (Y, 1))))
                if kind == FOUR:
                    between.update(among((6, 3, (IZ, 0))))
                if kind == MID:
                    for b in range(NBATCH):
                        between[2 + b, 0] = lambda b=b: rows_of(b, hn)
                        between[3 + b, 9] = lambda b=b: dct_columns(b, NBATCH * hn + b)
                for k in range(8):
                    tile(0, 0, k, i, n, s + 1 if kind != FIVE else 0, lo_done, parts + 2 * NP, between)
                    i += 1

            with pe.Fori(0, GROUPS - 1) as g:
                with pe.Fori(0, HALVES) as s:
                    step(g, s, MID)
                step(g, 4, FOUR)
                step(g, 5, FIVE)
            with pe.Fori(0, STEPS - 1) as s:
                step(GROUPS - 1, s, LAST_MID)
            step(GROUPS - 1, 5, LAST)


def kernel(**inputs):
    import numpy as _np
    import concourse.bacc as _bacc
    from concourse import mybir as _mybir
    from concourse.bass_utils import run_bass_kernel_spmd as _run

    pre = "L1_conv_"
    x = _np.ascontiguousarray(inputs["x"])
    w = [_np.transpose(inputs[pre + f"conv{k}_w"], (1, 2, 3, 0)) for k in (1, 2)]
    wt = _np.concatenate([_np.tile(v[1:].reshape(C, 9 * C), (4, 1)) for v in w], axis=1)
    w0 = _np.zeros((128, 256), _np.float32)
    w0[0:9] = _np.concatenate([_np.tile(v[0].reshape(9, C), (1, 4)) for v in w], axis=1)
    par = _np.tile(_np.stack([inputs[pre + k] for k in (
        "gn1_w", "gn1_b", "gn2_w", "gn2_b", "gn3_w", "gn3_b", "conv1_b", "conv2_b")], axis=1), (4, 1))
    dct, mats, coef, ind = constants()
    arrays = {"x": x, "wt": wt, "w0": w0, "par": par, "dct": dct, "mats": mats,
              "coef": coef.reshape(128, 1024), "ind": ind}
    nc = _bacc.Bacc("TRN2", target_bir_lowering=False, num_devices=1)
    feed, aps = {}, []
    for name, a in arrays.items():
        a = _np.ascontiguousarray(a)
        feed[f"in_{name}_dram"] = a
        aps.append(nc.dram_tensor(f"in_{name}_dram", a.shape, _mybir.dt.from_np(a.dtype), kind="ExternalInput").ap())
    B = x.shape[0]
    x1d = nc.dram_tensor("x1_dram", (B, C, H, 2, NA), _mybir.dt.float32, kind="Internal").ap()
    yd = nc.dram_tensor("y_dram", (B, C, H, 2, NA), _mybir.dt.float32, kind="Internal").ap()
    out = nc.dram_tensor("out_0_dram", x.shape, _mybir.dt.float32, kind="ExternalOutput").ap()
    build(nc, *aps, x1d, yd, out)
    r = _run(nc, [feed], core_ids=[0])
    return r.results[0]["out_0_dram"]
```
